# Optimizing a Trainium2 kernel written in Bass

```python
import numpy as np
import jax
import jax.numpy as jnp

def _softmax(x, axis=-1):
    return jax.nn.softmax(x, axis=axis)

def _gelu(x):
    return jax.nn.gelu(x, approximate=True)

def _silu(x):
    return jax.nn.silu(x)

def _sigmoid(x):
    return jax.nn.sigmoid(x)

def _layernorm(x, axis=-1, eps=1e-05):
    m = jnp.mean(x, axis=axis, keepdims=True)
    v = jnp.var(x, axis=axis, keepdims=True)
    return (x - m) / jnp.sqrt(v + eps)

def _scatter_add(tgt, idx, src, axis=0):
    return tgt.at[idx].add(src)

def _segment_sum(src, seg, n):
    return jax.ops.segment_sum(src, seg, n)
kernel_name = 'mk_adj_resnorm_d4_adj_r2_f84c0d'

def setup_inputs(seed: int=0):
    np.random.seed(seed)
    _w = jnp.asarray

    def _rec_inputs():
        import jax
        import jax.numpy as jnp
        _gk = jax.random.key(seed)
        x = -0.0005207 + 1.001 * jax.random.normal(jax.random.fold_in(_gk, 1), (4096, 128), jnp.float32)
        _a = jax.random.bernoulli(jax.random.fold_in(_gk, 2), 0.00390625, (4096, 4096))
        _a = jnp.logical_or(_a, jnp.eye(4096, dtype=bool))
        _af = _a.astype(jnp.float32)
        _af = _af * jax.random.uniform(jax.random.fold_in(_gk, 3), (4096, 4096), jnp.float32, 0.05, 0.00012207)
        adj = _af
        return (x, adj)
    x, adj = _rec_inputs()

    def _L0_gnn_setup():
        import jax, jax.numpy as jnp
        import numpy as np
        N_NODES = 4096
        D_FEAT = 128
        key = jax.random.key(seed)
        k1, k2, k3, k4, k5 = jax.random.split(key, 5)
        X = jax.random.normal(k1, (N_NODES, D_FEAT), dtype=jnp.float32)
        A_hat = jax.random.uniform(k2, (N_NODES, N_NODES), dtype=jnp.float32) / N_NODES
        w_global = jax.random.uniform(k3, (1,), dtype=jnp.float32)
        w_local = jax.random.uniform(k4, (N_NODES,), dtype=jnp.float32)
        W_agg = jax.random.normal(k5, (D_FEAT, D_FEAT), dtype=jnp.float32) / np.sqrt(D_FEAT)
        return {'X': X, 'A_hat': A_hat, 'w_global': w_global, 'w_local': w_local, 'W_agg': W_agg}
    _L0_gnn_all = _L0_gnn_setup()
    _L0_gnn_in = {k: v for k, v in _L0_gnn_all.items() if k in ('w_global', 'w_local', 'W_agg')}
    del _L0_gnn_all

    def _L1_gnn_setup():
        import jax, jax.numpy as jnp
        import numpy as np
        N = 4096
        D = 128
        DENSITY = 0.02
        key = jax.random.key(seed)
        k1, k2, k3, k4 = jax.random.split(key, 4)
        inputs = jax.random.normal(k1, (N, D), dtype=jnp.float32)
        vals = jax.random.uniform(k2, (N, N), dtype=jnp.float32, minval=0.1, maxval=1.0)
        mask = jax.random.uniform(k3, (N, N), dtype=jnp.float32) < DENSITY
        adj = jnp.where(mask, vals, 0.0)
        H_v = 0.1 * jax.random.normal(k4, (D, 1), dtype=jnp.float32)
        return {'inputs': inputs, 'adj': adj, 'H_v': H_v}
    _L1_gnn_all = _L1_gnn_setup()
    _L1_gnn_in = {k: v for k, v in _L1_gnn_all.items() if k in ('H_v',)}
    del _L1_gnn_all

    def _L2_gnn_setup():
        import jax, jax.numpy as jnp
        import numpy as np
        N = 10000
        D = 128
        F = 128
        K = F // 8
        key = jax.random.key(seed)
        k1, k2, k3, k4, k5 = jax.random.split(key, 5)
        h = jax.random.normal(k1, (N, D), dtype=jnp.float32)
        adj = jax.random.uniform(k2, (N, N), dtype=jnp.float32)
        W1 = jax.random.normal(k3, (D, K), dtype=jnp.float32) * 0.05
        W2 = jax.random.normal(k4, (K, D, F), dtype=jnp.float32) * 0.05
        b = jax.random.normal(k5, (K, F), dtype=jnp.float32) * 0.05
        return {'h': h, 'adj': adj, 'W1': W1, 'W2': W2, 'b': b}
    _L2_gnn_all = _L2_gnn_setup()
    _L2_gnn_in = {k: v for k, v in _L2_gnn_all.items() if k in ('W1', 'W2', 'b')}
    del _L2_gnn_all

    def _L3_gnn_setup():
        import jax, jax.numpy as jnp
        import numpy as np
        N_NODES = 8192
        D_FEAT = 128
        key = jax.random.key(seed)
        k1, k2, k3 = jax.random.split(key, 3)
        x = jax.random.normal(k1, (N_NODES, D_FEAT), dtype=jnp.float32)
        adj_matrix = jax.random.uniform(k2, (N_NODES, N_NODES), dtype=jnp.float32) / N_NODES
        W = jax.random.normal(k3, (D_FEAT, D_FEAT), dtype=jnp.float32) / np.sqrt(D_FEAT)
        b = jnp.zeros((D_FEAT,), dtype=jnp.float32)
        return {'x': x, 'adj_matrix': adj_matrix, 'W': W, 'b': b}
    _L3_gnn_all = _L3_gnn_setup()
    _L3_gnn_in = {k: v for k, v in _L3_gnn_all.items() if k in ('W', 'b')}
    del _L3_gnn_all
    return {'x': x, 'adj': adj, 'L0_gnn_w_global': _L0_gnn_in['w_global'], 'L0_gnn_w_local': _L0_gnn_in['w_local'], 'L0_gnn_W_agg': _L0_gnn_in['W_agg'], 'L1_gnn_H_v': _L1_gnn_in['H_v'], 'L2_gnn_W1': _L2_gnn_in['W1'], 'L2_gnn_W2': _L2_gnn_in['W2'], 'L2_gnn_b': _L2_gnn_in['b'], 'L3_gnn_W': _L3_gnn_in['W'], 'L3_gnn_b': _L3_gnn_in['b']}

def reference(x, adj, L0_gnn_w_global, L0_gnn_w_local, L0_gnn_W_agg, L1_gnn_H_v, L2_gnn_W1, L2_gnn_W2, L2_gnn_b, L3_gnn_W, L3_gnn_b):
    import jax
    import jax.numpy as jnp

    def _L0_gnn_ref(X, A_hat, w_global, w_local, W_agg):
        import jax, jax.numpy as jnp
        import numpy as np
        N_NODES = 4096
        D_FEAT = 128
        agg = jax.nn.relu(A_hat @ X @ W_agg)
        s = (jax.nn.sigmoid(w_global) * jax.nn.sigmoid(w_local))[:, None]
        return s * agg + X - s * X

    def _L1_gnn_ref(inputs, adj, H_v):
        import jax, jax.numpy as jnp
        import numpy as np
        N = 4096
        D = 128
        DENSITY = 0.02
        scores = jnp.squeeze(inputs @ H_v, -1)
        mask = adj != 0.0
        logits = adj * scores[None, :]
        neg = jnp.asarray(jnp.finfo(logits.dtype).min, logits.dtype)
        logits = jnp.where(mask, logits, neg)
        m = jnp.max(logits, axis=1, keepdims=True)
        e = jnp.where(mask, jnp.exp(logits - m), 0.0)
        s = jnp.sum(e, axis=1, keepdims=True)
        weights = e / jnp.where(s > 0, s, 1.0)
        return weights @ inputs

    def _L2_gnn_ref(h, adj, W1, W2, b):
        import jax, jax.numpy as jnp
        import numpy as np
        N = 10000
        D = 128
        F = 128
        K = F // 8
        node = h @ W1
        hw = jnp.einsum('nc,kcf->nkf', h, W2)
        x = jnp.einsum('nk,nkf->nf', node, hw)
        x = adj @ x
        x = x + node @ b
        return jax.nn.relu(x)

    def _L3_gnn_ref(x, adj_matrix, W, b):
        import jax, jax.numpy as jnp
        import numpy as np
        N_NODES = 8192
        D_FEAT = 128
        h = jnp.einsum('nd,ed->ne', x, W) + b
        return jnp.matmul(adj_matrix, h)
    x = _layernorm(x + _L0_gnn_ref(x, adj, L0_gnn_w_global, L0_gnn_w_local, L0_gnn_W_agg), axis=-1)
    x = _layernorm(x + _L1_gnn_ref(x, adj, L1_gnn_H_v), axis=-1)
    x = _layernorm(x + _L2_gnn_ref(x, adj, L2_gnn_W1, L2_gnn_W2, L2_gnn_b), axis=-1)
    x = _layernorm(x + _L3_gnn_ref(x, adj, L3_gnn_W, L3_gnn_b), axis=-1)
    return x

_drawn_inputs = setup_inputs


def setup_inputs(seed=0):
    import zlib

    import numpy as np

    out = dict(_drawn_inputs(seed))
    spreads = {'L3_gnn_b': (0.0, 0.1)}
    factors = {'L0_gnn_w_local': 8.0, 'L1_gnn_H_v': 4.178}
    for name, (base, spread) in spreads.items():
        noise = np.random.default_rng([zlib.crc32(name.encode()), seed]).standard_normal(out[name].shape)
        drawn = base * np.exp(spread * noise) if base else spread * noise
        out[name] = jnp.asarray(drawn.astype(out[name].dtype))
    for name, factor in factors.items():
        out[name] = (out[name] * factor).astype(out[name].dtype)
    return out
```

```python
from contextlib import ExitStack

import concourse.bass as bass
from concourse import mybir

F32 = mybir.dt.float32
BF16 = mybir.dt.bfloat16
ALU = mybir.AluOpType
ACT = mybir.ActivationFunctionType

P = 128
N = 4096
D = 128
TILES = N // P
GT = 4
GN = GT * P
GROUPS = N // GN
SLOT = 2048
RING = 8
CHUNKS = RING
K = 16
EPS = 1e-5
BIG = 2.0 ** 80


def build(nc, x, adj_rows, adj_cols, w_global, w_local, w_agg, h_v, w1, w2, b2, w3t, b3, out):
    with ExitStack() as ctx:
        def sb(name, shape, dt=F32):
            return ctx.enter_context(nc.sbuf_tensor(name, shape, dt))

        def sem(name):
            return ctx.enter_context(nc.semaphore(name))

        XA = sb("XA", [P, TILES * D])
        XB = sb("XB", [P, TILES * D])
        SG = sb("SG", [P, TILES * D])
        ring = sb("ring", [P, RING, SLOT])
        eT = sb("eT", [P, TILES, GN])
        prod = [eT[:, 4 * i:4 * i + 4, :].rearrange("p a (b f) -> p (a b) f", f=D) for i in range(2)]
        w2_sb = sb("w2_sb", [P, K * D])
        penalty = w2_sb[:, :].bitcast(BF16)
        acc_sb = sb("acc_sb", [P, 4, GN])
        y = sb("y", [P, GT, D])
        xn = sb("xn", [P, GT, D])
        xT_sb = sb("xT_sb", [P, GN])
        ident = sb("ident", [P, P])
        wagg_sb = sb("wagg_sb", [D, D])
        w3t_sb = sb("w3t_sb", [D, D])
        w1_sb = sb("w1_sb", [D, K])
        b2_sb = sb("b2_sb", [K, D])
        b3_sb = sb("b3_sb", [1, D])
        ones_row = sb("ones_row", [1, P])
        hv_sb = sb("hv_sb", [D, 1])
        hv_wide = sb("hv_wide", [D, P])
        gate = sb("gate", [P, TILES + 1])
        gate4 = sb("gate4", [P, GT])
        stats = sb("stats", [P, GT, 6])
        mv = sb("mv", [P, GT, 2])
        var4 = sb("var4", [P, GT])
        rstd = sb("rstd", [P, GT])
        minus_half = sb("minus_half", [P, GT])
        row_max = sb("row_max", [P, GT])
        neg_max = sb("neg_max", [P, GT])
        row_sum = sb("row_sum", [P, GT])
        has_edge = sb("has_edge", [P, GT])
        inv_sum = sb("inv_sum", [P, GT])
        node_all = sb("node_all", [P, TILES * K])
        node_cur = sb("node_cur", [P, 2, K])
        node4 = sb("node4", [P, GT * K])
        nodeT_sb = sb("nodeT_sb", [K, GN])

        acc = ctx.enter_context(nc.psum_tensor("acc", [P, 4, GN], F32))
        turn = ctx.enter_context(nc.psum_tensor("turn", [P, 2, GN], F32))
        nat = ctx.enter_context(nc.psum_tensor("nat", [P, GN], F32))
        xT = ctx.enter_context(nc.psum_tensor("xT", [P, GN], F32))
        nodeps = xT[:, 256:256 + K]

        landed = [sem(f"landed{i}") for i in range(RING)]
        x_landed = [sem(f"x_landed{i}") for i in range(4)]
        small_landed = sem("small_landed")
        w2_landed = sem("w2_landed")
        slot_free = sem("slot_free")
        stored = sem("stored")
        ident_zero = sem("ident_zero")
        consts = sem("consts")
        gate_exp = sem("gate_exp")
        gate_step = sem("gate_step")
        hv_ready = sem("hv_ready")
        acc_done = sem("acc_done")
        acc_saved = sem("acc_saved")
        nat_done = sem("nat_done")
        nat_read = sem("nat_read")
        y_part = sem("y_part")
        y_done = sem("y_done")
        stats_done = sem("stats_done")
        aggr_done = sem("aggr_done")
        var_done = sem("var_done")
        rstd_done = sem("rstd_done")
        x_done = sem("x_done")
        xT_done = sem("xT_done")
        xT_saved = sem("xT_saved")
        xn_kept = sem("xn_kept")
        small_done = sem("small_done")
        small_saved = sem("small_saved")
        pen_done = sem("pen_done")
        scaled = sem("scaled")
        max_done = sem("max_done")
        negmax_done = sem("negmax_done")
        exp_done = sem("exp_done")
        turned = sem("turned")
        evicted = sem("evicted")
        waited = sem("waited")
        edge_done = sem("edge_done")
        recip_done = sem("recip_done")
        inv_done = sem("inv_done")
        p_xT = sem("p_xT")
        p_xT_saved = sem("p_xT_saved")
        p_node = sem("p_node")
        p_node_saved = sem("p_node_saved")
        p_hw = sem("p_hw")
        p_hw_read = sem("p_hw_read")
        mix_done = sem("mix_done")
        node4_done = sem("node4_done")
        nodeT_done = sem("nodeT_done")
        nodeT_saved = sem("nodeT_saved")

        def tile(buf, t):
            return buf[:, t * D:(t + 1) * D]

        def group(buf, g):
            return buf[:, bass.ds(g * GN, GN)]

        def pair(r):
            return ring[:, 2 * r:2 * r + 2, :].rearrange("p a n -> p (a n)")

        def products(it, slots):
            return it * RING + slots

        block = ctx.enter_context(nc.Block())

        @block.sync
        def _(sp):
            def load(it, c, src, before="product"):
                if before == "product":
                    sp.wait_ge(slot_free, products(it - 1, c + 1))
                elif before == "turns":
                    sp.wait_ge(turned, (it - GROUPS - 1) * (GT * CHUNKS) + 4 * (c + 1))
                sp.dma_start(ring[:, c, :].rearrange("p (a n) -> p a n", a=src.shape[1]), src).then_inc(landed[c], 16)

            def columns(g, c):
                return adj_cols[g, :, c * SLOT:(c + 1) * SLOT].rearrange("p (a n) -> p a n", a=1) if isinstance(g, int) \
                    else adj_cols[bass.ds(g, 1), :, c * SLOT:(c + 1) * SLOT].rearrange("o p n -> p o n")

            def wide(t):
                cols = slice(t * GN, (t + 1) * GN) if isinstance(t, int) else bass.ds(t * GN, GN)
                return adj_cols[0:4, :, cols].rearrange("g p n -> p g n")

            def rows(t, half):
                return adj_rows[bass.ds(t, 1), :, half * SLOT:(half + 1) * SLOT].rearrange("o p n -> p o n")

            for c in range(CHUNKS):
                load(0, c, columns(0, c), before="nothing")
            with sp.Fori(1, GROUPS) as g:
                for c in range(CHUNKS):
                    load(g, c, columns(g, c))
            for c in range(CHUNKS):
                load(GROUPS, c, rows(c // 2, c % 2))
            with sp.Fori(1, GROUPS) as g:
                for c in range(CHUNKS):
                    load(g + GROUPS, c, rows(g * GT + c // 2, c % 2), before="turns")
            sp.wait_ge(max_done, TILES)
            sp.dma_start(w2_sb[:, :], w2).then_inc(w2_landed, 16)
            for layer in (2, 3):
                for c in range(CHUNKS):
                    if layer == 2:
                        load(2 * GROUPS, c, wide(c), before="turns")
                    else:
                        load((layer - 1) * GROUPS, c, wide(c))
                with sp.Fori(1, 4) as m:
                    for c in range(CHUNKS):
                        load(m + (layer - 1) * GROUPS, c, wide(m * CHUNKS + c))
                with sp.Fori(4, GROUPS) as g:
                    for c in range(CHUNKS):
                        load(g + (layer - 1) * GROUPS, c, columns(g, c))
            with sp.Fori(0, GROUPS) as g:
                sp.wait_ge(x_done, g + (3 * GROUPS + 1))
                sp.dma_start(out[bass.ds(g, 1), :, :, :].rearrange("o t p d -> p (o t) d"),
                             group(XA, g).rearrange("p (t d) -> p t d", d=D)).then_inc(stored, 16)
            sp.wait_ge(stored, 16 * GROUPS)

        @block.gpsimd
        def _(pool):
            pool.memset(ident[:, :], 0.0).then_inc(ident_zero, 1)
            pool.memset(minus_half[:, :], -0.5).then_inc(consts, 1)
            pool.memset(ones_row[:, :], 1.0).then_inc(consts, 1)
            pool.wait_ge(ident_zero, 1)
            pool.affine_select(out=ident[:, :], in_=ident[:, :], compare_op=ALU.not_equal, fill=1.0, base=0,
                               pattern=[[-1, P]], channel_multiplier=1).then_inc(consts, 1)
            pool.wait_ge(consts, 3)
            with pool.Fori(0, 4 * GROUPS) as e:
                pool.wait_ge(var_done, e + 1)
                pool.tensor_tensor(rstd[:, :], var4[:, :], minus_half[:, :], ALU.pow).then_inc(rstd_done, 1)

        @block.scalar
        def _(act):
            for i in range(4):
                w = TILES * D // 4
                act.dma_start(XA[:, i * w:(i + 1) * w], x[:, i * w:(i + 1) * w]).then_inc(x_landed[i], 16)
            for dst, src in ((gate[:, 0:TILES], w_local), (gate[:, TILES:TILES + 1], w_global), (wagg_sb[:, :], w_agg),
                             (hv_sb[:, :], h_v), (w1_sb[:, :], w1), (b2_sb[:, :], b2), (w3t_sb[:, :], w3t),
                             (b3_sb[:, :], b3)):
                act.dma_start(dst, src).then_inc(small_landed, 16)
            act.wait_ge(small_landed, 16 * 8)
            act.activation(gate[:, :], gate[:, :], ACT.Exp, scale=-1.0).then_inc(gate_exp, 1)

            def save_acc(complete, value, bank, k=0, turned_back=None):
                act.wait_ge(complete, value)
                if turned_back is not None:
                    act.wait_ge(nat_done, turned_back)
                act.activation(acc_sb[:, k, :], bank, ACT.Copy).then_inc(acc_saved, 1)

            def save_xT(n):
                act.wait_ge(xT_done, n + 1)
                act.wait_ge(small_done, n)
                act.activation(xT_sb[:, :], xT[:, :], ACT.Copy).then_inc(xT_saved, 1)

            def keep_xn(e, dst):
                act.wait_ge(x_done, e + 1)
                act.activation(dst, xn[:, :, :].rearrange("p t d -> p (t d)"), ACT.Copy).then_inc(xn_kept, 1)

            def bank_of(b):
                return acc[:, bass.ds(b, 1), :].rearrange("p o n -> p (o n)")

            def layer0(g, first=False):
                save_acc(slot_free, products(g, RING), acc[:, 0, :] if first else bank_of(g % 4),
                         turned_back=None if first else g)
                keep_xn(g, group(XB, g))
                act.wait_ge(xT_done, g + 1)
                if not first:
                    act.wait_ge(small_done, g)
                act.activation(xT_sb[:, :], xT[:, :], ACT.Copy).then_inc(xT_saved, 1)
                act.wait_ge(small_done, g + 1)
                act.activation(group(SG, g), turn[:, 0, :], ACT.Copy, scale=1.0 / BIG).then_inc(small_saved, 1)

            layer0(0, first=True)
            with act.Fori(1, GROUPS) as g:
                layer0(g)

            def exponential(g, r, first=False):
                act.wait_ge(negmax_done, g * GT + (r + 1))
                if r == 0 and not first:
                    act.wait_ge(inv_done, g)
                act.activation(pair(r), pair(r), ACT.Exp, bias=neg_max[:, r:r + 1], scale=BIG,
                               accum_out=row_sum[:, r:r + 1]).then_inc(exp_done, 1)

            def evict(g, r):
                for c in range(CHUNKS):
                    act.wait_ge(turned, g * (GT * CHUNKS) + (r * CHUNKS + c + 1))
                    act.activation(eT[:, 4 * c:4 * c + 4, r * P:(r + 1) * P],
                                   turn[:, c % 2, :].rearrange("p (a n) -> p a n", a=4), ACT.Copy).then_inc(evicted, 1)

            def layer1(g, first=False, last=False):
                for r in range(GT):
                    if r < GT - 1:
                        exponential(g, r + 1)
                    elif not last:
                        exponential(g + 1, 0)
                    evict(g, r)
                    if r == 0 and not first:
                        save_acc(acc_done, g, bank_of((g + 3) % 4), turned_back=g + (GROUPS - 1))

            exponential(0, 0, first=True)
            layer1(0, first=True)
            with act.Fori(1, GROUPS - 1) as g:
                layer1(g)
            layer1(GROUPS - 1, last=True)
            save_acc(acc_done, GROUPS, acc[:, 3, :], turned_back=2 * GROUPS - 1)

            act.wait_ge(p_xT, 1)
            act.activation(xT_sb[:, 0:P], xT[:, 0:P], ACT.Copy).then_inc(p_xT_saved, 1)
            with act.Fori(1, TILES) as t:
                act.wait_ge(p_xT, t + 1)
                act.wait_ge(p_hw, t * 4)
                act.activation(xT_sb[:, 0:P], xT[:, 0:P], ACT.Copy).then_inc(p_xT_saved, 1)

            def layer2(g, first=False):
                if not first:
                    act.wait_ge(nodeT_done, g)
                act.activation(node4[:, :], node_all[:, bass.ds(g * (GT * K), GT * K)], ACT.Copy).then_inc(node4_done, 1)
                save_acc(slot_free, products(GROUPS + 3, RING), bank_of(g), turned_back=g + 2 * GROUPS)
                act.wait_ge(nodeT_done, g + 1)
                act.wait_ge(nat_done, g + 2 * GROUPS)
                act.activation(nodeT_sb[:, :], xT[0:K, :], ACT.Copy).then_inc(nodeT_saved, 1)

            def layer2_rest(g):
                keep_xn(g + 2 * GROUPS, group(XA, g))
                save_xT(g + GROUPS)
                act.wait_ge(small_done, g + (GROUPS + 1))
                act.activation(group(XB, g), turn[:, 0, :], ACT.Copy).then_inc(small_saved, 1)

            layer2(0, first=True)
            layer2_rest(0)
            with act.Fori(1, 4) as g:
                layer2(g)
                layer2_rest(g)
            act.wait_ge(nat_done, 2 * GROUPS + 4)
            for k in range(4):
                save_acc(slot_free, products(GROUPS + 4 + k, RING), acc[:, k, :], k)
            for g in range(4, GROUPS):
                act.wait_ge(nodeT_done, g)
                act.activation(node4[:, :], node_all[:, g * GT * K:(g + 1) * GT * K], ACT.Copy).then_inc(node4_done, 1)
                act.wait_ge(nodeT_done, g + 1)
                act.wait_ge(nat_done, g + 2 * GROUPS)
                act.activation(nodeT_sb[:, :], xT[0:K, :], ACT.Copy).then_inc(nodeT_saved, 1)
                layer2_rest(g)

            with act.Fori(0, 4) as g:
                save_acc(slot_free, products(2 * GROUPS + 3, RING), bank_of(g), turned_back=g + 3 * GROUPS)
            act.wait_ge(nat_done, 3 * GROUPS + 4)
            for k in range(4):
                save_acc(slot_free, products(2 * GROUPS + 4 + k, RING), acc[:, k, :], k)

        @block.tensor
        def _(pe):
            pe.wait_ge(consts, 3)

            def group_chunk(it, e, c, stationary, bank):
                if c == 0 and e is not None:
                    pe.wait_ge(acc_saved, e - 3)
                pe.wait_ge(landed[c], (it + 1) * 16)
                for a in range(4):
                    t = 4 * c + a
                    mm = pe.matmul(bank, tile(stationary, t), ring[:, c, a * GN:(a + 1) * GN],
                                   start=(t == 0), stop=(t == TILES - 1))
                mm.then_inc(slot_free, 1)

            def turn_back(e, k, weight, extra=False):
                pe.wait_ge(acc_saved, e + 1)
                if not (isinstance(e, int) and e == 0):
                    pe.wait_ge(nat_read, e)
                for q in range(GT):
                    mm = pe.matmul(nat[:, q * D:(q + 1) * D], acc_sb[:, k, q * P:(q + 1) * P], weight[:, :],
                                   start=True, stop=not extra)
                    if extra:
                        mm = pe.matmul(nat[:, q * D:(q + 1) * D], nodeT_sb[:, q * P:(q + 1) * P], b2_sb[:, :],
                                       start=False, stop=True)
                mm.then_inc(nat_done, 1)

            def turn_x(e, n):
                pe.wait_ge(x_done, e + 1)
                for q in range(GT):
                    mm = pe.transpose(xT[:, q * P:(q + 1) * P], xn[:, q, :], ident[:, :])
                mm.then_inc(xT_done, 1)

            def scores(g):
                pe.wait_ge(xT_saved, g + 1)
                if not (isinstance(g, int) and g == 0):
                    pe.wait_ge(small_saved, g)
                pe.matmul(turn[:, 0, :], hv_wide[:, :], xT_sb[:, :], start=True, stop=True).then_inc(small_done, 1)

            pe.wait_ge(small_landed, 16 * 8)
            pe.wait_ge(hv_ready, 1)
            for c in range(CHUNKS):
                if c % 2 == 0:
                    pe.wait_ge(x_landed[c // 2], 16)
                group_chunk(0, None, c, XA, acc[:, 0, :])

            def layer0(g, four_ago):
                bank = acc[:, bass.ds(g % 4, 1), :].rearrange("p o n -> p (o n)")
                for c in range(CHUNKS):
                    if c == 0 and four_ago:
                        pe.wait_ge(acc_saved, g - 3)
                    group_chunk(g, None, c, XA, bank)
                    if c == 1:
                        turn_back(g - 1, 0, wagg_sb)
                    if c == 4:
                        turn_x(g - 1, g - 1)
                    if c == 6:
                        scores(g - 1)

            with pe.Fori(1, 4) as g:
                layer0(g, four_ago=False)
            with pe.Fori(4, GROUPS) as g:
                layer0(g, four_ago=True)
            turn_back(GROUPS - 1, 0, wagg_sb)
            turn_x(GROUPS - 1, GROUPS - 1)
            scores(GROUPS - 1)
            pe.wait_ge(small_saved, GROUPS)

            def turn_rows(g, r, c):
                if c == 0:
                    pe.wait_ge(exp_done, g * GT + (r + 1))
                if not (isinstance(g, int) and g == 0 and r == 0 and c < 2):
                    pe.wait_ge(evicted, g * (GT * CHUNKS) + (r * CHUNKS + c - 1))
                for a in range(4):
                    mm = pe.transpose(turn[:, c % 2, a * P:(a + 1) * P],
                                      pair(r)[:, (4 * c + a) * P:(4 * c + a + 1) * P], ident[:, :])
                mm.then_inc(turned, 1)

            def weigh(g, c, bank):
                if c == 0:
                    pe.wait_ge(acc_saved, g + (GROUPS - 3))
                pe.wait_ge(evicted, g * (GT * CHUNKS) + ((GT - 1) * CHUNKS + c + 1))
                for a in range(4):
                    t = 4 * c + a
                    mm = pe.matmul(bank, tile(XB, t), eT[:, t, :], start=(t == 0), stop=(t == TILES - 1))
                if c == CHUNKS - 1:
                    mm.then_inc(acc_done, 1)

            def layer1(g, first=False):
                for r in range(GT):
                    for c in range(CHUNKS):
                        if r == 0 and not first:
                            weigh(g - 1, c, acc[:, bass.ds((g + 3) % 4, 1), :].rearrange("p o n -> p (o n)"))
                        turn_rows(g, r, c)
                    if r == 1 and not first:
                        turn_back(g + (GROUPS - 1), 0, ident)

            pe.wait_ge(xn_kept, GROUPS)
            layer1(0, first=True)
            with pe.Fori(1, GROUPS) as g:
                layer1(g)
            for c in range(CHUNKS):
                weigh(GROUPS - 1, c, acc[:, 3, :])

            def turn_tile(t):
                if t >= TILES - GT:
                    pe.wait_ge(x_done, 2 * GROUPS)
                elif t == 0:
                    pe.wait_ge(x_done, 2 * GROUPS - 1)
                if t >= 1:
                    pe.wait_ge(p_xT_saved, t)
                pe.transpose(xT[:, 0:P], tile(XA, t), ident[:, :]).then_inc(p_xT, 1)

            def node(t):
                pe.wait_ge(p_xT_saved, t + 1)
                if t >= 1:
                    pe.wait_ge(p_node_saved, t)
                pe.matmul(nodeps, xT_sb[:, 0:P], w1_sb[:, :], start=True, stop=True).then_inc(p_node, 1)

            def bases(t, c):
                n = 4 * t + c
                if n >= 2:
                    pe.wait_ge(p_hw_read, n - 1)
                pe.matmul(turn[:, c % 2, :], xT_sb[:, 0:P], w2_sb[:, c * GN:(c + 1) * GN],
                          start=True, stop=True).then_inc(p_hw, 1)

            pe.wait_ge(evicted, TILES * CHUNKS)
            pe.wait_ge(w2_landed, 16)
            for t in range(2):
                turn_tile(t)
                node(t)
                for c in range(4):
                    bases(t, c)
            turn_back(2 * GROUPS - 1, 0, ident)
            for t in range(TILES):
                if t + 2 < TILES:
                    turn_tile(t + 2)
                pe.wait_ge(landed[t % RING], 16 * (2 * GROUPS + t // RING + 1))
                pe.wait_ge(mix_done, t + 1)
                for k in range(4):
                    mm = pe.matmul(acc[:, k, :], tile(SG, t), ring[:, t % RING, k * GN:(k + 1) * GN],
                                   start=(t == 0), stop=(t == TILES - 1))
                    if k == 3:
                        mm.then_inc(slot_free, 1)
                    if t + 2 < TILES:
                        if k == 0:
                            node(t + 2)
                        bases(t + 2, k)

            def turn_node(g):
                pe.wait_ge(node4_done, g + 1)
                if not isinstance(g, int):
                    pe.wait_ge(xT_saved, g + GROUPS)
                for q in range(GT):
                    mm = pe.transpose(xT[0:K, q * P:(q + 1) * P], node4[:, q * K:(q + 1) * K], ident[:, :])
                mm.then_inc(nodeT_done, 1)

            def project(g):
                pe.wait_ge(xT_saved, g + (GROUPS + 1))
                pe.wait_ge(small_saved, g + GROUPS)
                for q in range(GT):
                    pe.matmul(turn[:, 0, q * D:(q + 1) * D], xT_sb[:, q * P:(q + 1) * P], w3t_sb[:, :],
                              start=True, stop=False)
                    mm = pe.matmul(turn[:, 0, q * D:(q + 1) * D], ones_row[:, :], b3_sb[:, :],
                                   start=False, stop=True)
                mm.then_inc(small_done, 1)

            with pe.Fori(4, GROUPS) as g:
                bank = acc[:, bass.ds(g - 4, 1), :].rearrange("p o n -> p (o n)")
                for c in range(CHUNKS):
                    group_chunk(g + 2 * GROUPS, g + 2 * GROUPS, c, SG, bank)
                    if c == 0:
                        turn_node(g - 4)
                    if c == 1:
                        pe.wait_ge(nodeT_saved, g - 3)
                        turn_back(g + (2 * GROUPS - 4), 0, ident, extra=True)
                    if c == 4:
                        turn_x(g + (2 * GROUPS - 4), 0)
                    if c == 6:
                        project(g - 4)

            pe.wait_ge(acc_saved, 3 * GROUPS)
            for t in range(TILES):
                if 3 <= t <= 12 and t % 3 == 0:
                    project(3 + t // 3)
                if t < 12:
                    g = 4 + t // 3
                    if t % 3 == 0:
                        turn_node(g)
                        pe.wait_ge(nodeT_saved, g + 1)
                        turn_back(g + 2 * GROUPS, g - 4, ident, extra=True)
                    if t % 3 == 2:
                        turn_x(g + 2 * GROUPS, 0)
                pe.wait_ge(small_saved, GROUPS + t // GT + 1)
                pe.wait_ge(landed[t % RING], 16 * (3 * GROUPS + t // RING + 1))
                for k in range(4):
                    mm = pe.matmul(acc[:, k, :], tile(XB, t), ring[:, t % RING, k * GN:(k + 1) * GN],
                                   start=(t == 0), stop=(t == TILES - 1))
                    if k == 3:
                        mm.then_inc(slot_free, 1)
            with pe.Fori(4, GROUPS) as g:
                bank = acc[:, bass.ds(g - 4, 1), :].rearrange("p o n -> p (o n)")
                for c in range(CHUNKS):
                    group_chunk(g + 3 * GROUPS, g + 3 * GROUPS, c, XB, bank)
                    if c == 2:
                        turn_back(g + (3 * GROUPS - 4), 0, ident)
            for k in range(4):
                turn_back(3 * GROUPS + 4 + k, k, ident)

        @block.vector
        def _(dve):
            flat_y = y[:, :, :].rearrange("p t d -> p (t d)")

            def normalise(e, dst):
                for q in range(GT):
                    bn = dve.bn_stats(stats[:, q, :], y[:, q, :])
                bn.then_inc(stats_done, 1)
                dve.wait_ge(stats_done, e + 1)
                dve.sem_inc(waited, 1)
                for q in range(GT):
                    bn = dve.bn_aggr(mv[:, q, :], stats[:, q, :])
                bn.then_inc(aggr_done, 1)
                dve.wait_ge(aggr_done, e + 1)
                dve.tensor_scalar(var4[:, :], mv[:, :, 1], EPS, None, ALU.add).then_inc(var_done, 1)
                dve.wait_ge(rstd_done, e + 1)
                for q in range(GT):
                    ts = dve.tensor_scalar(dst(q), y[:, q, :], mv[:, q, 0:1], rstd[:, q:q + 1],
                                           ALU.subtract, ALU.mult)
                ts.then_inc(x_done, 1)

            def in_xn(q):
                return xn[:, q, :]

            dve.wait_ge(small_landed, 16 * 8)
            dve.tensor_copy(hv_wide[:, :], hv_sb[:, 0:1].to_broadcast([D, P])).then_inc(hv_ready, 1)
            dve.wait_ge(gate_exp, 1)
            dve.tensor_scalar(gate[:, :], gate[:, :], 1.0, None, ALU.add).then_inc(gate_step, 1)
            dve.wait_ge(gate_step, 1)
            dve.reciprocal(gate[:, :], gate[:, :]).then_inc(gate_step, 1)
            dve.wait_ge(gate_step, 2)
            dve.tensor_scalar(gate[:, 0:TILES], gate[:, 0:TILES], gate[:, TILES:TILES + 1], None,
                              ALU.mult).then_inc(gate_step, 1)
            dve.wait_ge(gate_step, 3)

            def layer0(g, first=False):
                dve.tensor_copy(gate4[:, :], gate[:, bass.ds(g * GT, GT)]).then_inc(y_part, 1)
                dve.wait_ge(nat_done, g + 1)
                dve.scalar_tensor_tensor(out=flat_y, in0=nat[:, :], scalar=0.0, in1=group(XA, g),
                                         op0=ALU.max, op1=ALU.subtract).then_inc(nat_read, 1)
                dve.wait_ge(nat_read, g + 1)
                dve.wait_ge(y_part, g * 2 + 1)
                for q in range(GT):
                    ts = dve.tensor_scalar(y[:, q, :], y[:, q, :], gate4[:, q:q + 1], None, ALU.mult)
                ts.then_inc(y_part, 1)
                dve.wait_ge(y_part, g * 2 + 2)
                dve.scalar_tensor_tensor(out=flat_y, in0=group(XA, g), scalar=2.0, in1=flat_y,
                                         op0=ALU.mult, op1=ALU.add).then_inc(y_done, 1)
                if not first:
                    dve.wait_ge(xn_kept, g)
                dve.wait_ge(y_done, g + 1)
                normalise(g, in_xn)

            layer0(0, first=True)
            with dve.Fori(1, GROUPS) as g:
                layer0(g)

            def logits(g, r, first=False):
                if r % 4 == 0 and first:
                    dve.wait_ge(small_saved, GROUPS)
                n = g * GT + r
                for half in range(2):
                    dve.wait_ge(landed[2 * r + half], (g + GROUPS + 1) * 16)
                if not first:
                    dve.wait_ge(max_done, n)
                dve.tensor_scalar(penalty, pair(r), 0.0, -1.0, ALU.is_equal, ALU.mult).then_inc(pen_done, 1)
                dve.tensor_tensor(pair(r), pair(r), SG[:, :], ALU.mult).then_inc(scaled, 1)
                dve.wait_ge(pen_done, n + 1)
                dve.wait_ge(scaled, n + 1)
                dve.sem_inc(waited, 1)
                dve.tensor_tensor_reduce(pair(r), pair(r), penalty, 1.0, -3.0e38, ALU.add, ALU.max,
                                         row_max[:, r:r + 1]).then_inc(max_done, 1)
                dve.wait_ge(max_done, n + 1)
                if not (first or (isinstance(g, int) and g == 0)):
                    dve.wait_ge(exp_done, n - (GT - 1))
                dve.tensor_scalar(neg_max[:, r:r + 1], row_max[:, r:r + 1], -BIG, None,
                                  ALU.mult).then_inc(negmax_done, 1)

            def edges(g):
                if not (isinstance(g, int) and g == 0):
                    dve.wait_ge(inv_done, g)
                dve.tensor_scalar(has_edge[:, :], row_max[:, :], -0.5, None, ALU.is_gt).then_inc(edge_done, 1)

            def inverse(g):
                dve.wait_ge(exp_done, g * GT + GT)
                dve.wait_ge(edge_done, g + 1)
                dve.reciprocal(inv_sum[:, :], row_sum[:, :]).then_inc(recip_done, 1)
                dve.wait_ge(recip_done, g + 1)
                dve.tensor_tensor(inv_sum[:, :], inv_sum[:, :], has_edge[:, :], ALU.mult).then_inc(inv_done, 1)

            def finish1(g):
                e = g + GROUPS
                dve.wait_ge(x_done, e)
                dve.wait_ge(nat_done, e + 1)
                dve.wait_ge(inv_done, g + 1)
                for q in range(GT):
                    st = dve.scalar_tensor_tensor(out=y[:, q, :], in0=nat[:, q * D:(q + 1) * D],
                                                  scalar=inv_sum[:, q:q + 1], in1=XB[:, bass.ds(g * GN + q * D, D)],
                                                  op0=ALU.mult, op1=ALU.add)
                st.then_inc(nat_read, 1)
                dve.wait_ge(nat_read, e + 1)
                normalise(e, lambda q: XA[:, bass.ds(g * GN + q * D, D)])

            dve.wait_ge(xn_kept, GROUPS)
            logits(0, 0, first=True)
            for r in range(1, GT):
                logits(0, r)
            edges(0)

            def layer1(g):
                logits(g, 0)
                inverse(g - 1)
                for r in range(1, GT):
                    logits(g, r)
                edges(g)
                finish1(g - 1)

            with dve.Fori(1, GROUPS) as g:
                layer1(g)
            inverse(GROUPS - 1)

            def mixture(t):
                dve.wait_ge(p_node, t + 1)
                dve.tensor_copy(node_cur[:, 0, :], nodeps)
                dve.tensor_copy(node_all[:, bass.ds(t * K, K)], nodeps).then_inc(p_node_saved, 1)
                dve.wait_ge(p_node_saved, t + 1)
                for c in range(4):
                    dve.wait_ge(p_hw, t * 4 + (c + 1))
                    dve.tensor_tensor(prod[0][:, 4 * c:4 * c + 4, :],
                                      turn[:, c % 2, :].rearrange("p (k f) -> p k f", k=4),
                                      node_cur[:, 0, 4 * c:4 * c + 4].rearrange("p (k o) -> p k o", o=1).to_broadcast([P, 4, D]),
                                      ALU.mult).then_inc(p_hw_read, 1)
                dve.wait_ge(p_hw_read, t * 4 + 4)
                dve.tensor_reduce(SG[:, bass.ds(t * D, D)], prod[0].rearrange("p k f -> p f k"),
                                  mybir.AxisListType.X, ALU.add).then_inc(mix_done, 1)

            dve.wait_ge(acc_done, GROUPS)
            mixture(0)
            mixture(1)
            finish1(GROUPS - 1)
            with dve.Fori(2, TILES) as t:
                mixture(t)

            def finish2(g):
                e = g + 2 * GROUPS
                dve.wait_ge(nat_done, e + 1)
                dve.scalar_tensor_tensor(out=flat_y, in0=nat[:, :], scalar=0.0, in1=group(XA, g),
                                         op0=ALU.max, op1=ALU.add).then_inc(nat_read, 1)
                dve.wait_ge(nat_read, e + 1)
                dve.wait_ge(xT_done, g + GROUPS)
                dve.wait_ge(xn_kept, g + GROUPS)
                normalise(e, in_xn)

            with dve.Fori(0, GROUPS) as g:
                finish2(g)

            def finish3(g):
                e = g + 3 * GROUPS
                dve.wait_ge(x_done, e)
                dve.wait_ge(nat_done, e + 1)
                dve.tensor_tensor(flat_y, nat[:, :], group(XA, g), ALU.add).then_inc(nat_read, 1)
                dve.wait_ge(nat_read, e + 1)
                normalise(e, lambda q: XA[:, bass.ds(g * GN + q * D, D)])

            dve.wait_ge(xn_kept, 2 * GROUPS)
            with dve.Fori(0, GROUPS) as g:
                finish3(g)


_OUT = (GROUPS, GT, P, D)


def kernel(**inputs):
    import numpy as np
    import concourse.bacc as bacc
    from concourse.bass_utils import run_bass_kernel_spmd as run

    a = {k: np.asarray(v) for k, v in inputs.items()}
    adj = a["adj"]
    laid = {
        "x": a["x"].reshape(TILES, P, D).transpose(1, 0, 2).reshape(P, TILES * D),
        "adj_rows": adj.reshape(TILES, P, N),
        "adj_cols": adj.reshape(GROUPS, GN, TILES, P).transpose(0, 3, 2, 1).reshape(GROUPS, P, TILES * GN),
        "w_global": np.broadcast_to(a["L0_gnn_w_global"].reshape(1, 1), (P, 1)),
        "w_local": a["L0_gnn_w_local"].reshape(TILES, P).T,
        "w_agg": a["L0_gnn_W_agg"],
        "h_v": a["L1_gnn_H_v"],
        "w1": a["L2_gnn_W1"],
        "w2": a["L2_gnn_W2"].transpose(1, 0, 2).reshape(D, K * D),
        "b2": a["L2_gnn_b"],
        "w3t": a["L3_gnn_W"].T,
        "b3": a["L3_gnn_b"].reshape(1, D),
    }
    nc = bacc.Bacc("TRN2", target_bir_lowering=False, num_devices=1)
    arrays, args = {}, []
    for name, value in laid.items():
        value = np.ascontiguousarray(value)
        arrays[f"in_{name}"] = value
        args.append(nc.dram_tensor(f"in_{name}", value.shape, mybir.dt.from_np(value.dtype), kind="ExternalInput").ap())
    args.append(nc.dram_tensor("out", _OUT, F32, kind="ExternalOutput").ap())
    build(nc, *args)
    r = run(nc, [arrays], core_ids=[0])
    return r.results[0]["out"].reshape(N, D)
```

```python
from contextlib import ExitStack

import concourse.bass as bass
from concourse import mybir

F32 = mybir.dt.float32
F32R = mybir.dt.float32r
BF16 = mybir.dt.bfloat16
ALU = mybir.AluOpType
ACT = mybir.ActivationFunctionType

P = 128
N = 4096
D = 128
TILES = N // P
GT = 4
GN = GT * P
GROUPS = N // GN
SLOT = 2048
RING = 8
PN = 2 * P
CUT = SLOT // 2
ROUND = 2 * RING
CHUNKS = RING
K = 16
EPS = 1e-5
BIG = 2.0 ** 80


def build(nc, x, adj_rows, adj_cols, w_global, w_local, w_agg, h_v, w1, w2, b2, w3t, b3, out):
    with ExitStack() as ctx:
        def sb(name, shape, dt=F32):
            return ctx.enter_context(nc.sbuf_tensor(name, shape, dt))

        def sem(name):
            return ctx.enter_context(nc.semaphore(name))

        KB = 1024
        arena = nc.sbuf_usable_end // 32 * 32 - 176 * KB

        def place(name, at_kb, shape, dt=F32):
            return nc.alloc_sbuf_tensor_at(name, shape, dt, offset=arena + at_kb * KB)

        XA = place("XA", 0, [P, TILES * D])
        XB = place("XB", 16, [P, TILES * D])
        SG = place("SG", 32, [P, TILES * D])
        h_hi = place("h_hi", 16, [P, TILES * D], F32R)
        h_lo = place("h_lo", 32, [P, TILES * D], F32R)
        ring = place("ring", 48, [P, RING, SLOT])
        eT = place("eT", 112, [P, 2, TILES, PN])
        a_hi = place("a_hi", 112, [P, 4, CUT], F32R)
        a_lo = place("a_lo", 128, [P, 4, CUT], F32R)
        w2_hi = place("w2_hi", 112, [D, K * D], F32R)
        w2_lo = place("w2_lo", 120, [D, K * D], F32R)
        terms = place("terms", 128, [P, K, D])
        s_hi = place("s_hi", 144, [P, TILES * D], F32R)
        s_lo = place("s_lo", 160, [P, TILES * D], F32R)

        w2_sb = sb("w2_sb", [P, K * D])
        penalty = w2_sb[:, :].bitcast(BF16)
        acc_sb = sb("acc_sb", [P, 4, GN])
        y = sb("y", [P, GT, D])
        xn = sb("xn", [P, GT, D])
        xT_sb = sb("xT_sb", [P, GN])
        tT_hi = sb("tT_hi", [P, 2, P], F32R)
        tT_lo = sb("tT_lo", [P, 2, P], F32R)
        ident = sb("ident", [P, P])
        wagg_sb = sb("wagg_sb", [D, D])
        w3t_sb = sb("w3t_sb", [D, D])
        w1_sb = sb("w1_sb", [D, K])
        w1_hi = sb("w1_hi", [D, K], F32R)
        w1_lo = sb("w1_lo", [D, K], F32R)
        b2_sb = sb("b2_sb", [K, D])
        b3_sb = sb("b3_sb", [1, D])
        ones_row = sb("ones_row", [1, P])
        hv_sb = sb("hv_sb", [D, 1])
        hv_wide = sb("hv_wide", [D, P])
        gate = sb("gate", [P, TILES + 1])
        gate4 = sb("gate4", [P, GT])
        stats = sb("stats", [P, GT, 6])
        mv = sb("mv", [P, GT, 2])
        var4 = sb("var4", [P, GT])
        rstd = sb("rstd", [P, GT])
        minus_half = sb("minus_half", [P, GT])
        row_max = sb("row_max", [P, GT])
        neg_max = sb("neg_max", [P, GT])
        row_sum = sb("row_sum", [P, GT])
        has_edge = sb("has_edge", [P, GT])
        inv_sum = sb("inv_sum", [P, GT])
        node_all = sb("node_all", [P, TILES * K])
        node_cur = sb("node_cur", [P, K])
        node4 = sb("node4", [P, GT * K])
        nodeT_sb = w2_sb[0:K, 0:GN]

        assert nc.sbuf_base <= arena

        acc = ctx.enter_context(nc.psum_tensor("acc", [P, 4, GN], F32))
        turn = ctx.enter_context(nc.psum_tensor("turn", [P, 2, GN], F32))
        nat = ctx.enter_context(nc.psum_tensor("nat", [P, GN], F32))
        xT = ctx.enter_context(nc.psum_tensor("xT", [P, GN], F32))
        nodeps = nat[:, 0:K]

        landed = [sem(f"landed{i}") for i in range(RING)]
        x_landed = [sem(f"x_landed{i}") for i in range(CHUNKS)]
        small_landed = sem("small_landed")
        w2_landed = sem("w2_landed")
        stored = sem("stored")
        hi_done = sem("hi_done")
        lo_done = sem("lo_done")
        used = sem("used")
        x_hi_done = sem("x_hi_done")
        x_lo_done = sem("x_lo_done")
        ident_zero = sem("ident_zero")
        consts = sem("consts")
        gate_exp = sem("gate_exp")
        gate_step = sem("gate_step")
        hv_ready = sem("hv_ready")
        w1_hi_done = sem("w1_hi_done")
        w1_cut = sem("w1_cut")
        acc_saved = sem("acc_saved")
        nat_done = sem("nat_done")
        nat_read = sem("nat_read")
        y_part = sem("y_part")
        y_done = sem("y_done")
        stats_done = sem("stats_done")
        aggr_done = sem("aggr_done")
        var_done = sem("var_done")
        rstd_done = sem("rstd_done")
        x_done = sem("x_done")
        xT_done = sem("xT_done")
        xT_saved = sem("xT_saved")
        xn_kept = sem("xn_kept")
        small_done = sem("small_done")
        small_saved = sem("small_saved")
        h_lo_done = sem("h_lo_done")
        pen_done = sem("pen_done")
        scaled = sem("scaled")
        max_done = sem("max_done")
        negmax_done = sem("negmax_done")
        exp_done = sem("exp_done")
        turned = sem("turned")
        evicted = sem("evicted")
        weighed = sem("weighed")
        waited = sem("waited")
        edge_done = sem("edge_done")
        recip_done = sem("recip_done")
        inv_done = sem("inv_done")
        w2_hi_done = sem("w2_hi_done")
        w2_cut = sem("w2_cut")
        p_xT = sem("p_xT")
        p_hi = sem("p_hi")
        p_lo = sem("p_lo")
        p_node = sem("p_node")
        p_node_saved = sem("p_node_saved")
        p_hw = sem("p_hw")
        p_hw_read = sem("p_hw_read")
        mix_done = sem("mix_done")
        mix_hi = sem("mix_hi")
        mix_lo = sem("mix_lo")
        node4_done = sem("node4_done")
        nodeT_done = sem("nodeT_done")
        nodeT_saved = sem("nodeT_saved")

        CUT2 = GROUPS * ROUND
        CUT3 = CUT2 + 4 * ROUND
        USED2 = CUT2
        USED2B = USED2 + TILES
        USED3 = USED2B + 4 * ROUND

        def cols(buf, start, width):
            return buf[:, start:start + width] if isinstance(start, int) else buf[:, bass.ds(start, width)]

        def tile(buf, t):
            return cols(buf, t * D, D)

        def group(buf, g):
            return cols(buf, g * GN, GN)

        def bank_of(b):
            return acc[:, b, :] if isinstance(b, int) else acc[:, bass.ds(b, 1), :].rearrange("p o n -> p (o n)")

        def pair(r):
            return ring[:, 2 * r:2 * r + 2, :].rearrange("p a n -> p (a n)")

        block = ctx.enter_context(nc.Block())

        @block.sync
        def _(sp):
            def load(c, src, n, after=None, value=None):
                if after is not None:
                    sp.wait_ge(after, value)
                sp.dma_start(ring[:, c, :].rearrange("p (a n) -> p a n", a=src.shape[1]), src).then_inc(landed[c], 16)

            def columns(g, c):
                if isinstance(g, int):
                    return adj_cols[g:g + 1, :, c * SLOT:(c + 1) * SLOT].rearrange("o p n -> p o n")
                return adj_cols[bass.ds(g, 1), :, c * SLOT:(c + 1) * SLOT].rearrange("o p n -> p o n")

            def wide(t):
                part = slice(t * GN, (t + 1) * GN) if isinstance(t, int) else bass.ds(t * GN, GN)
                return adj_cols[0:4, :, part].rearrange("g p n -> p g n")

            def rows(t, half):
                return adj_rows[bass.ds(t, 1), :, half * SLOT:(half + 1) * SLOT].rearrange("o p n -> p o n")

            for c in range(CHUNKS):
                sp.dma_start(group(XA, c), group(x, c)).then_inc(x_landed[c], 16)
                load(c, columns(0, c), 0)
            with sp.Fori(1, GROUPS) as g:
                for c in range(CHUNKS):
                    load(c, columns(g, c), g, lo_done, g * ROUND + (2 * (c + 1) - ROUND))
            for c in range(CHUNKS):
                load(c, rows(c // 2, c % 2), GROUPS, lo_done, (GROUPS - 1) * ROUND + 2 * (c + 1))
            with sp.Fori(1, GROUPS) as g:
                for c in range(CHUNKS):
                    load(c, rows(g * GT + c // 2, c % 2), g + GROUPS, turned, (g - 1) * (GT * CHUNKS) + 4 * (c + 1))
            sp.wait_ge(max_done, TILES)
            sp.dma_start(w2_sb[:, :], w2).then_inc(w2_landed, 16)
            for c in range(CHUNKS):
                load(c, wide(c), 16, turned, (GROUPS - 1) * (GT * CHUNKS) + 4 * (c + 1))
            with sp.Fori(1, 4) as m:
                for c in range(CHUNKS):
                    load(c, wide(m * CHUNKS + c), m + 16, used, (m - 1) * RING + (USED2 + c + 1))
            for c in range(CHUNKS):
                load(c, columns(4, c), 20, used, 3 * RING + (USED2 + c + 1))
            with sp.Fori(5, GROUPS) as g:
                for c in range(CHUNKS):
                    load(c, columns(g, c), g + 16, lo_done, (g - 5) * ROUND + (CUT2 + 2 * (c + 1)))
            with sp.Fori(0, 4) as m:
                for c in range(CHUNKS):
                    load(c, wide(m * CHUNKS + c), m + 24, lo_done, m * ROUND + (CUT3 - ROUND + 2 * (c + 1)))
            with sp.Fori(4, GROUPS) as g:
                for c in range(CHUNKS):
                    load(c, columns(g, c), g + 24, lo_done, g * ROUND + (CUT3 - ROUND + 2 * (c + 1)))
            with sp.Fori(0, GROUPS) as g:
                sp.wait_ge(x_done, g + (3 * GROUPS + 1))
                sp.dma_start(out[bass.ds(g, 1), :, :, :].rearrange("o t p d -> p (o t) d"),
                             group(XA, g).rearrange("p (t d) -> p t d", d=D)).then_inc(stored, 16)
            sp.wait_ge(stored, 16 * GROUPS)

        @block.gpsimd
        def _(pool):
            pool.memset(ident[:, :], 0.0).then_inc(ident_zero, 1)
            pool.memset(minus_half[:, :], -0.5).then_inc(consts, 1)
            pool.memset(ones_row[:, :], 1.0).then_inc(consts, 1)
            pool.wait_ge(ident_zero, 1)
            pool.affine_select(out=ident[:, :], in_=ident[:, :], compare_op=ALU.not_equal, fill=1.0, base=0,
                               pattern=[[-1, P]], channel_multiplier=1).then_inc(consts, 1)
            pool.wait_ge(consts, 3)
            with pool.Fori(0, 4 * GROUPS) as e:
                pool.wait_ge(var_done, e + 1)
                pool.tensor_tensor(rstd[:, :], var4[:, :], minus_half[:, :], ALU.pow).then_inc(rstd_done, 1)

        @block.scalar
        def _(act):
            for dst, src in ((wagg_sb[:, :], w_agg), (gate[:, 0:TILES], w_local), (gate[:, TILES:TILES + 1], w_global),
                             (hv_sb[:, :], h_v), (w1_sb[:, :], w1), (b2_sb[:, :], b2), (w3t_sb[:, :], w3t),
                             (b3_sb[:, :], b3)):
                act.dma_start(dst, src).then_inc(small_landed, 16)

            def high(c, rounds, before):
                act.wait_ge(landed[c], rounds * 16)
                for h in range(2):
                    if before is not None and not (isinstance(before, int) and before + h < 4):
                        act.wait_ge(used, before + (h - 3))
                    act.activation(a_hi[:, (2 * c + h) % 4, :], ring[:, c, h * CUT:(h + 1) * CUT],
                                   ACT.Copy).then_inc(hi_done, 1)

            def save_acc(complete, value, bank, k=0, turned_back=None):
                act.wait_ge(complete, value)
                if turned_back is not None:
                    act.wait_ge(nat_done, turned_back)
                act.activation(acc_sb[:, k, :], bank, ACT.Copy).then_inc(acc_saved, 1)

            def keep_xn(e, dst):
                act.wait_ge(x_done, e + 1)
                act.activation(dst, xn[:, :, :].rearrange("p t d -> p (t d)"), ACT.Copy).then_inc(xn_kept, 1)

            def save_xT(n, first=False):
                act.wait_ge(xT_done, n + 1)
                if not first:
                    act.wait_ge(small_done, n)
                act.activation(xT_sb[:, :], xT[:, :], ACT.Copy).then_inc(xT_saved, 1)

            def save_scores(g):
                act.wait_ge(small_done, g + 1)
                act.activation(group(SG, g), turn[:, 0, :], ACT.Copy, scale=1.0 / BIG).then_inc(small_saved, 1)

            for c in range(CHUNKS):
                act.wait_ge(x_landed[c], 16)
                act.activation(group(s_hi, c), group(XA, c), ACT.Copy).then_inc(x_hi_done, 1)
                high(c, 1, 2 * c)
            act.wait_ge(small_landed, 16 * 8)
            act.activation(gate[:, :], gate[:, :], ACT.Exp, scale=-1.0).then_inc(gate_exp, 1)
            act.activation(w1_hi[:, :], w1_sb[:, :], ACT.Copy).then_inc(w1_hi_done, 1)

            def layer0(g):
                first = isinstance(g, int)
                for c in range(CHUNKS):
                    high(c, g + 1, g * ROUND + 2 * c)
                    if c == 1:
                        save_acc(used, g * ROUND, bank_of(0 if first else (g - 1) % 4),
                                 turned_back=None if first else g - 1)
                        if not first:
                            save_scores(g - 2)
                    if c == 6:
                        keep_xn(g - 1, group(XB, g - 1))
                    if c == 7:
                        save_xT(g - 1, first=first)

            layer0(1)
            with act.Fori(2, GROUPS) as g:
                layer0(g)
            last = GROUPS - 1
            save_acc(used, GROUPS * ROUND, bank_of(last % 4), turned_back=last)
            save_scores(last - 1)
            save_xT(last)
            save_scores(last)
            keep_xn(last, group(XB, last))

            def exponential(g, r, first=False):
                act.wait_ge(negmax_done, g * GT + (r + 1))
                if r == 0 and not first:
                    act.wait_ge(inv_done, g)
                act.activation(pair(r), pair(r), ACT.Exp, bias=neg_max[:, r:r + 1], scale=BIG,
                               accum_out=row_sum[:, r:r + 1]).then_inc(exp_done, 1)

            def evict(g, r):
                for c in range(CHUNKS):
                    act.wait_ge(turned, g * (GT * CHUNKS) + (r * CHUNKS + c + 1))
                    act.activation(eT[:, r // 2, 4 * c:4 * c + 4, (r % 2) * P:(r % 2 + 1) * P],
                                   turn[:, c % 2, :].rearrange("p (a n) -> p a n", a=4), ACT.Copy).then_inc(evicted, 1)

            def layer1(g, first=False, last=False):
                for r in range(GT):
                    if r < GT - 1:
                        exponential(g, r + 1)
                    elif not last:
                        exponential(g + 1, 0)
                    evict(g, r)
                    if r == 1 and not first:
                        save_acc(weighed, g * 2, bank_of((g + 3) % 4), turned_back=g + (GROUPS - 1))

            exponential(0, 0, first=True)
            layer1(0, first=True)
            with act.Fori(1, GROUPS - 1) as g:
                layer1(g)
            layer1(GROUPS - 1, last=True)

            act.wait_ge(w2_landed, 16)
            act.wait_ge(weighed, 2 * GROUPS - 1)
            act.activation(w2_hi[:, :], w2_sb[:, :], ACT.Copy).then_inc(w2_hi_done, 1)

            def tile_high(t, b):
                act.wait_ge(p_xT, t + 1)
                if not (isinstance(t, int) and t < 2):
                    act.wait_ge(p_hw, t * 4 - 4)
                act.activation(tT_hi[:, b, :], xT[:, 0:P], ACT.Copy).then_inc(p_hi, 1)

            def mixture_high(t):
                act.wait_ge(mix_done, t + 1)
                act.activation(tile(s_hi, t), tile(SG, t), ACT.Copy).then_inc(mix_hi, 1)

            tile_high(0, 0)
            tile_high(1, 1)
            save_acc(weighed, 2 * GROUPS, acc[:, 3, :], turned_back=2 * GROUPS - 1)
            with act.Fori(1, TILES // 2) as u:
                for b in range(2):
                    tile_high(u * 2 + b, b)
                    mixture_high(u * 2 + (b - 2))
            mixture_high(TILES - 2)
            mixture_high(TILES - 1)

            def node_in(g, first=False):
                if not first:
                    act.wait_ge(nodeT_done, g)
                act.activation(node4[:, :], cols(node_all, g * (GT * K), GT * K), ACT.Copy).then_inc(node4_done, 1)

            def node_turned(g):
                act.wait_ge(nodeT_done, g + 1)
                act.wait_ge(nat_done, g + 2 * GROUPS)
                act.activation(nodeT_sb[:, :], xT[0:K, :], ACT.Copy).then_inc(nodeT_saved, 1)

            def h_high(g):
                act.wait_ge(small_done, g + (GROUPS + 1))
                act.activation(group(h_hi, g), turn[:, 0, :], ACT.Copy).then_inc(small_saved, 1)

            def layer2(g):
                first = isinstance(g, int)
                for c in range(CHUNKS):
                    high(c, g + 17, None if first and c < 2 else (g - 4) * ROUND + (USED2B + 2 * c))
                    if c == 0:
                        node_in(g - 4, first=first)
                    if c == 1:
                        save_acc(used, USED2B, bank_of(g - 4), turned_back=g - 4 + 2 * GROUPS)
                        node_turned(g - 4)
                        if not first:
                            h_high(g - 5)
                    if c == 6:
                        keep_xn(g - 4 + 2 * GROUPS, group(XA, g - 4))
                    if c == 7:
                        save_xT(g - 4 + GROUPS)

            act.wait_ge(mix_done, TILES)
            layer2(4)
            with act.Fori(5, GROUPS) as g:
                layer2(g)

            act.wait_ge(nat_done, 2 * GROUPS + 4)
            for k in range(3):
                save_acc(used, USED2B + (k + 1) * ROUND, acc[:, k, :], k)
            for t in range(2 * RING):
                high(t % RING, 25 + t // RING, USED3 + 2 * t)
                k = 4 + t // 4
                if t == 1:
                    save_acc(used, USED3, acc[:, 3, :], 3)
                if t % 4 == 0:
                    h_high(k - 1)
                    node_in(k)
                if t % 4 == 1:
                    node_turned(k)
                if t % 4 == 3:
                    keep_xn(k + 2 * GROUPS, group(XA, k))
                    save_xT(k + GROUPS)
            h_high(7)
            with act.Fori(2, 4) as m:
                for c in range(CHUNKS):
                    high(c, m + 25, m * ROUND + (USED3 + 2 * c))
            with act.Fori(4, GROUPS - 1) as g:
                for c in range(CHUNKS):
                    high(c, g + 25, g * ROUND + (USED3 + 2 * c))
                    if c in (1, 4):
                        e = (g - 4) * 2 + c // 4
                        save_acc(used, g * ROUND + USED3, bank_of(e % 4), c // 4, turned_back=e + (3 * GROUPS - 1))
            for c in range(CHUNKS):
                high(c, GROUPS - 1 + 25, (GROUPS - 1) * ROUND + (USED3 + 2 * c))
                if c == 1:
                    save_acc(used, USED3 + 7 * ROUND, acc[:, 2, :], 2)
            save_acc(used, USED3 + 8 * ROUND, acc[:, 3, :], 3)

        @block.tensor
        def _(pe):
            pe.wait_ge(consts, 3)

            def three(dst, x_hi, x_lo, m_hi, m_lo, start, stop):
                pe.matmul(dst, x_hi, m_hi, start=start, stop=False)
                pe.matmul(dst, x_hi, m_lo, start=False, stop=False)
                return pe.matmul(dst, x_lo, m_hi, start=False, stop=stop)

            def group_chunk(cut, c, hi, lo, bank):
                for h in range(2):
                    pe.wait_ge(lo_done, cut + (h + 1))
                    b = (2 * c + h) % 4
                    for a in range(2):
                        t = 4 * c + 2 * h + a
                        mm = three(bank, tile(hi, t), tile(lo, t), a_hi[:, b, a * GN:(a + 1) * GN],
                                   a_lo[:, b, a * GN:(a + 1) * GN], t == 0, t == TILES - 1)
                    mm.then_inc(used, 1)

            def turn_back(e, k, weight, extra=False):
                pe.wait_ge(acc_saved, e + 1)
                if not (isinstance(e, int) and e == 0):
                    pe.wait_ge(nat_read, e)
                for q in range(GT):
                    mm = pe.matmul(nat[:, q * D:(q + 1) * D], acc_sb[:, k, q * P:(q + 1) * P], weight[:, :],
                                   start=True, stop=not extra)
                    if extra:
                        mm = pe.matmul(nat[:, q * D:(q + 1) * D], nodeT_sb[:, q * P:(q + 1) * P], b2_sb[:, :],
                                       start=False, stop=True)
                mm.then_inc(nat_done, 1)

            def turn_x(e):
                pe.wait_ge(x_done, e + 1)
                for q in range(GT):
                    mm = pe.transpose(xT[:, q * P:(q + 1) * P], xn[:, q, :], ident[:, :])
                mm.then_inc(xT_done, 1)

            def scores(g):
                pe.wait_ge(xT_saved, g + 1)
                if not (isinstance(g, int) and g == 0):
                    pe.wait_ge(small_saved, g)
                pe.matmul(turn[:, 0, :], hv_wide[:, :], xT_sb[:, :], start=True, stop=True).then_inc(small_done, 1)

            for c in range(CHUNKS):
                pe.wait_ge(x_lo_done, c + 1)
                group_chunk(2 * c, c, s_hi, s_lo, acc[:, 0, :])
            pe.wait_ge(small_landed, 16 * 8)
            pe.wait_ge(hv_ready, 1)

            def layer0(g, four_ago=True):
                if four_ago:
                    pe.wait_ge(acc_saved, g - 3)
                for c in range(CHUNKS):
                    group_chunk(g * ROUND + 2 * c, c, s_hi, s_lo, bank_of(g % 4))
                    if c == 1:
                        turn_back(g - 1, 0, wagg_sb)
                    if c == 6:
                        turn_x(g - 1)
                    if c == 7:
                        scores(g - 1)

            layer0(1, four_ago=False)
            with pe.Fori(2, 4) as g:
                layer0(g, four_ago=False)
            with pe.Fori(4, GROUPS) as g:
                layer0(g)
            turn_back(GROUPS - 1, 0, wagg_sb)
            turn_x(GROUPS - 1)
            scores(GROUPS - 1)
            pe.wait_ge(small_saved, GROUPS)

            def turn_rows(g, r, c):
                if c == 0:
                    pe.wait_ge(exp_done, g * GT + (r + 1))
                if not (isinstance(g, int) and g == 0 and r == 0 and c < 2):
                    pe.wait_ge(evicted, g * (GT * CHUNKS) + (r * CHUNKS + c - 1))
                for a in range(4):
                    mm = pe.transpose(turn[:, c % 2, a * P:(a + 1) * P],
                                      pair(r)[:, (4 * c + a) * P:(4 * c + a + 1) * P], ident[:, :])
                mm.then_inc(turned, 1)

            def weigh(g, half, ts, bank):
                for t in ts:
                    if t == 0 and half == 0:
                        pe.wait_ge(acc_saved, g + (GROUPS - 3))
                    if t % 4 == 0:
                        pe.wait_ge(evicted, g * (GT * CHUNKS) + ((2 * half + 1) * CHUNKS + t // 4 + 1))
                    mm = pe.matmul(bank[:, half * PN:(half + 1) * PN], tile(XB, t), eT[:, half, t, :],
                                   start=(t == 0), stop=(t == TILES - 1))
                    if t == TILES - 1:
                        mm.then_inc(weighed, 1)

            def layer1(g, first=False):
                for r in range(GT):
                    for c in range(CHUNKS):
                        turn_rows(g, r, c)
                        ts = range((r % 2) * 16 + 2 * c, (r % 2) * 16 + 2 * c + 2)
                        if r < 2 and not first:
                            weigh(g - 1, 1, ts, bank_of((g + 3) % 4))
                        if r >= 2:
                            weigh(g, 0, ts, bank_of(g % 4))
                    if r == 2 and not first:
                        turn_back(g + (GROUPS - 1), 0, ident)

            pe.wait_ge(xn_kept, GROUPS)
            layer1(0, first=True)
            with pe.Fori(1, GROUPS) as g:
                layer1(g)

            def turn_tile(t):
                if t >= TILES - GT:
                    pe.wait_ge(x_done, 2 * GROUPS)
                elif t == 0:
                    pe.wait_ge(x_done, 2 * GROUPS - 2)
                elif t == TILES - 2 * GT:
                    pe.wait_ge(x_done, 2 * GROUPS - 1)
                if t >= 1:
                    pe.wait_ge(p_lo, t)
                pe.transpose(xT[:, 0:P], tile(XA, t), ident[:, :]).then_inc(p_xT, 1)

            def node(t):
                pe.wait_ge(p_lo, t + 1)
                if t >= 1:
                    pe.wait_ge(p_node_saved, t)
                if t == 0:
                    pe.wait_ge(nat_read, 2 * GROUPS - 1)
                if t == 2:
                    pe.wait_ge(nat_read, 2 * GROUPS)
                three(nodeps, tT_hi[:, t % 2, :], tT_lo[:, t % 2, :], w1_hi[:, :], w1_lo[:, :], True, True).then_inc(p_node, 1)

            def bases(t, c):
                n = 4 * t + c
                if n >= 2:
                    pe.wait_ge(p_hw_read, n - 1)
                part = slice(c * GN, (c + 1) * GN)
                three(turn[:, c % 2, :], tT_hi[:, t % 2, :], tT_lo[:, t % 2, :], w2_hi[:, part], w2_lo[:, part],
                      True, True).then_inc(p_hw, 1)

            turn_tile(0)
            weigh(GROUPS - 1, 1, range(TILES), acc[:, 3, :])
            pe.wait_ge(w1_cut, 1)
            pe.wait_ge(w2_cut, 1)
            for t in range(2):
                if t == 0:
                    turn_tile(1)
                node(t)
                for c in range(4):
                    bases(t, c)
            pe.wait_ge(p_node_saved, 2)
            turn_back(2 * GROUPS - 1, 0, ident)
            turn_tile(2)
            for t in range(TILES):
                if t + 3 < TILES:
                    turn_tile(t + 3)
                pe.wait_ge(landed[t % RING], 16 * (2 * GROUPS + t // RING + 1))
                pe.wait_ge(mix_done, t + 1)
                for k in range(4):
                    mm = pe.matmul(acc[:, k, :], tile(SG, t), ring[:, t % RING, k * GN:(k + 1) * GN],
                                   start=(t == 0), stop=(t == TILES - 1))
                    if k == 3:
                        mm.then_inc(used, 1)
                    if t + 2 < TILES:
                        if k == 0:
                            node(t + 2)
                        bases(t + 2, k)

            def turn_node(g):
                pe.wait_ge(node4_done, g + 1)
                pe.wait_ge(xT_saved, g + GROUPS)
                for q in range(GT):
                    mm = pe.transpose(xT[0:K, q * P:(q + 1) * P], node4[:, q * K:(q + 1) * K], ident[:, :])
                mm.then_inc(nodeT_done, 1)

            def project(g):
                pe.wait_ge(xT_saved, g + (GROUPS + 1))
                pe.wait_ge(small_saved, g + GROUPS)
                if not (isinstance(g, int) and g == 0):
                    pe.wait_ge(h_lo_done, g)
                for q in range(GT):
                    pe.matmul(turn[:, 0, q * D:(q + 1) * D], xT_sb[:, q * P:(q + 1) * P], w3t_sb[:, :],
                              start=True, stop=False)
                    mm = pe.matmul(turn[:, 0, q * D:(q + 1) * D], ones_row[:, :], b3_sb[:, :],
                                   start=False, stop=True)
                mm.then_inc(small_done, 1)

            def layer2(g):
                for c in range(CHUNKS):
                    if c == 0:
                        turn_node(g - 4)
                        pe.wait_ge(acc_saved, g + (2 * GROUPS - 3))
                    group_chunk((g - 4) * ROUND + (CUT2 + 2 * c), c, s_hi, s_lo, bank_of(g - 4))
                    if c == 1:
                        pe.wait_ge(nodeT_saved, g - 3)
                        turn_back(g + (2 * GROUPS - 4), 0, ident, extra=True)
                    if c == 6:
                        turn_x(g + (2 * GROUPS - 4))
                    if c == 7:
                        project(g - 4)

            pe.wait_ge(mix_lo, TILES)
            layer2(4)
            with pe.Fori(5, GROUPS) as g:
                layer2(g)

            pe.wait_ge(acc_saved, 3 * GROUPS)
            for t in range(TILES):
                k = 4 + t // 4
                if t % 4 == 0 and 4 <= t <= 16:
                    project(k - 1)
                if k < GROUPS:
                    if t % 4 == 0:
                        turn_node(k)
                    if t % 4 == 1:
                        pe.wait_ge(nodeT_saved, k + 1)
                        turn_back(k + 2 * GROUPS, k - 4, ident, extra=True)
                    if t % 4 == 3:
                        turn_x(k + 2 * GROUPS)
                if t % 4 == 0:
                    pe.wait_ge(h_lo_done, t // GT + 1)
                for h in range(2):
                    pe.wait_ge(lo_done, CUT3 + 2 * t + h + 1)
                    for a, (still, moving) in enumerate(((h_hi, a_hi), (h_hi, a_lo), (h_lo, a_hi))):
                        for b in range(2):
                            mm = pe.matmul(acc[:, 2 * h + b, :], tile(still, t),
                                           moving[:, (2 * t + h) % 4, b * GN:(b + 1) * GN],
                                           start=(t == 0 and a == 0), stop=(t == TILES - 1 and a == 2))
                    mm.then_inc(used, 1)
            with pe.Fori(4, GROUPS - 1) as g:
                for c in range(CHUNKS):
                    if c == 0:
                        pe.wait_ge(acc_saved, (g - 4) * 2 + (3 * GROUPS + 1))
                    group_chunk(g * ROUND + (CUT3 + 2 * c), c, h_hi, h_lo, bank_of(g - 4))
                    if c in (2, 5):
                        turn_back((g - 4) * 2 + (3 * GROUPS + c // 4), c // 4, ident)
            for c in range(CHUNKS):
                group_chunk((GROUPS - 1) * ROUND + (CUT3 + 2 * c), c, h_hi, h_lo, acc[:, 3, :])
                if c == 2:
                    turn_back(3 * GROUPS + 6, 2, ident)
            turn_back(3 * GROUPS + 7, 3, ident)

        @block.vector
        def _(dve):
            flat_y = y[:, :, :].rearrange("p t d -> p (t d)")

            def low(c, cut):
                for h in range(2):
                    b = (2 * c + h) % 4
                    dve.wait_ge(hi_done, cut + (h + 1))
                    dve.tensor_tensor(a_lo[:, b, :], ring[:, c, h * CUT:(h + 1) * CUT], a_hi[:, b, :].bitcast(F32),
                                      ALU.subtract).then_inc(lo_done, 1)

            def norm_stats(e):
                for q in range(GT):
                    bn = dve.bn_stats(stats[:, q, :], y[:, q, :])
                bn.then_inc(stats_done, 1)

            def norm_var(e):
                dve.wait_ge(stats_done, e + 1)
                dve.sem_inc(waited, 1)
                for q in range(GT):
                    bn = dve.bn_aggr(mv[:, q, :], stats[:, q, :])
                bn.then_inc(aggr_done, 1)
                dve.wait_ge(aggr_done, e + 1)
                dve.tensor_scalar(var4[:, :], mv[:, :, 1], EPS, None, ALU.add).then_inc(var_done, 1)

            def norm_out(e, dst):
                dve.wait_ge(rstd_done, e + 1)
                for q in range(GT):
                    ts = dve.tensor_scalar(dst(q), y[:, q, :], mv[:, q, 0:1], rstd[:, q:q + 1],
                                           ALU.subtract, ALU.mult)
                ts.then_inc(x_done, 1)

            def in_xn(q):
                return xn[:, q, :]

            def in_place(g):
                return lambda q: cols(XA, g * GN + q * D, D)

            for c in range(CHUNKS):
                dve.wait_ge(x_hi_done, c + 1)
                dve.tensor_tensor(group(s_lo, c), group(XA, c), group(s_hi, c).bitcast(F32),
                                  ALU.subtract).then_inc(x_lo_done, 1)
                low(c, 2 * c)
            dve.wait_ge(small_landed, 16 * 8)
            dve.tensor_copy(hv_wide[:, :], hv_sb[:, 0:1].to_broadcast([D, P])).then_inc(hv_ready, 1)
            dve.wait_ge(w1_hi_done, 1)
            dve.tensor_tensor(w1_lo[:, :], w1_sb[:, :], w1_hi[:, :].bitcast(F32), ALU.subtract).then_inc(w1_cut, 1)
            dve.wait_ge(gate_exp, 1)
            dve.tensor_scalar(gate[:, :], gate[:, :], 1.0, None, ALU.add).then_inc(gate_step, 1)
            dve.wait_ge(gate_step, 1)
            dve.reciprocal(gate[:, :], gate[:, :]).then_inc(gate_step, 1)
            dve.wait_ge(gate_step, 2)
            dve.tensor_scalar(gate[:, 0:TILES], gate[:, 0:TILES], gate[:, TILES:TILES + 1], None,
                              ALU.mult).then_inc(gate_step, 1)
            dve.wait_ge(gate_step, 3)

            def residual0(g):
                dve.tensor_copy(gate4[:, :], cols(gate, g * GT, GT)).then_inc(y_part, 1)
                dve.wait_ge(nat_done, g + 1)
                dve.scalar_tensor_tensor(out=flat_y, in0=nat[:, :], scalar=0.0, in1=group(XA, g),
                                         op0=ALU.max, op1=ALU.subtract).then_inc(nat_read, 1)
                dve.wait_ge(nat_read, g + 1)
                dve.wait_ge(y_part, g * 2 + 1)
                for q in range(GT):
                    ts = dve.tensor_scalar(y[:, q, :], y[:, q, :], gate4[:, q:q + 1], None, ALU.mult)
                ts.then_inc(y_part, 1)

            def stats0(g):
                dve.wait_ge(y_part, g * 2 + 2)
                dve.scalar_tensor_tensor(out=flat_y, in0=group(XA, g), scalar=2.0, in1=flat_y,
                                         op0=ALU.mult, op1=ALU.add).then_inc(y_done, 1)
                dve.wait_ge(y_done, g + 1)
                norm_stats(g)

            def layer0(g):
                first = isinstance(g, int)
                for c in range(CHUNKS):
                    low(c, g * ROUND + 2 * c)
                    if c == 2:
                        residual0(g - 1)
                    if c == 3:
                        stats0(g - 1)
                    if c == 4:
                        norm_var(g - 1)
                    if c == 5:
                        if not first:
                            dve.wait_ge(xn_kept, g - 1)
                        norm_out(g - 1, in_xn)

            layer0(1)
            with dve.Fori(2, GROUPS) as g:
                layer0(g)
            residual0(GROUPS - 1)
            stats0(GROUPS - 1)
            norm_var(GROUPS - 1)
            dve.wait_ge(xn_kept, GROUPS - 1)
            norm_out(GROUPS - 1, in_xn)

            def logits(g, r):
                n = g * GT + r
                for half in range(2):
                    dve.wait_ge(landed[2 * r + half], (g + GROUPS + 1) * 16)
                if not (isinstance(g, int) and g == 0 and r == 0):
                    dve.wait_ge(max_done, n)
                dve.tensor_scalar(penalty, pair(r), 0.0, -1.0, ALU.is_equal, ALU.mult).then_inc(pen_done, 1)
                if isinstance(g, int) and g == 0 and r == 0:
                    dve.wait_ge(small_saved, GROUPS)
                dve.tensor_tensor(pair(r), pair(r), SG[:, :], ALU.mult).then_inc(scaled, 1)
                dve.wait_ge(pen_done, n + 1)
                dve.wait_ge(scaled, n + 1)
                dve.sem_inc(waited, 1)
                dve.tensor_tensor_reduce(pair(r), pair(r), penalty, 1.0, -3.0e38, ALU.add, ALU.max,
                                         row_max[:, r:r + 1]).then_inc(max_done, 1)
                dve.wait_ge(max_done, n + 1)
                if not (isinstance(g, int) and g == 0):
                    dve.wait_ge(exp_done, n - (GT - 1))
                dve.tensor_scalar(neg_max[:, r:r + 1], row_max[:, r:r + 1], -BIG, None,
                                  ALU.mult).then_inc(negmax_done, 1)

            def edges(g):
                if not (isinstance(g, int) and g == 0):
                    dve.wait_ge(inv_done, g)
                dve.tensor_scalar(has_edge[:, :], row_max[:, :], -0.5, None, ALU.is_gt).then_inc(edge_done, 1)

            def inverse(g):
                dve.wait_ge(exp_done, g * GT + GT)
                dve.wait_ge(edge_done, g + 1)
                dve.reciprocal(inv_sum[:, :], row_sum[:, :]).then_inc(recip_done, 1)
                dve.wait_ge(recip_done, g + 1)
                dve.tensor_tensor(inv_sum[:, :], inv_sum[:, :], has_edge[:, :], ALU.mult).then_inc(inv_done, 1)

            def finish1(g):
                e = g + GROUPS
                dve.wait_ge(x_done, e)
                dve.wait_ge(nat_done, e + 1)
                for q in range(GT):
                    st = dve.scalar_tensor_tensor(out=y[:, q, :], in0=nat[:, q * D:(q + 1) * D],
                                                  scalar=inv_sum[:, q:q + 1], in1=cols(XB, g * GN + q * D, D),
                                                  op0=ALU.mult, op1=ALU.add)
                st.then_inc(nat_read, 1)
                dve.wait_ge(nat_read, e + 1)
                norm_stats(e)
                norm_var(e)
                norm_out(e, in_place(g))

            for r in range(GT):
                logits(0, r)
            edges(0)
            logits(1, 0)
            inverse(0)
            for r in range(1, GT):
                logits(1, r)
            edges(1)
            dve.wait_ge(xn_kept, GROUPS)
            with dve.Fori(2, GROUPS) as g:
                logits(g, 0)
                finish1(g - 2)
                inverse(g - 1)
                for r in range(1, GT):
                    logits(g, r)
                edges(g)
            finish1(GROUPS - 2)
            inverse(GROUPS - 1)

            dve.wait_ge(w2_hi_done, 1)
            dve.tensor_tensor(w2_lo[:, :], w2_sb[:, :], w2_hi[:, :].bitcast(F32), ALU.subtract).then_inc(w2_cut, 1)

            def tile_low(t, b):
                dve.wait_ge(p_hi, t + 1)
                dve.tensor_tensor(tT_lo[:, b, :], xT[:, 0:P], tT_hi[:, b, :].bitcast(F32),
                                  ALU.subtract).then_inc(p_lo, 1)

            def mixture_terms(t):
                if not (isinstance(t, int) and t == 0):
                    dve.wait_ge(mix_done, t)
                dve.wait_ge(p_node, t + 1)
                dve.tensor_copy(node_cur[:, :], nodeps)
                dve.tensor_copy(cols(node_all, t * K, K), nodeps).then_inc(p_node_saved, 1)
                dve.wait_ge(p_node_saved, t + 1)
                for c in range(4):
                    dve.wait_ge(p_hw, t * 4 + (c + 1))
                    dve.tensor_tensor(terms[:, 4 * c:4 * c + 4, :],
                                      turn[:, c % 2, :].rearrange("p (k f) -> p k f", k=4),
                                      node_cur[:, 4 * c:4 * c + 4].rearrange("p (k o) -> p k o", o=1).to_broadcast([P, 4, D]),
                                      ALU.mult).then_inc(p_hw_read, 1)

            def mixture_sum(t):
                dve.wait_ge(p_hw_read, t * 4 + 4)
                dve.tensor_reduce(tile(SG, t), terms[:, :, :].rearrange("p k f -> p f k"),
                                  mybir.AxisListType.X, ALU.add).then_inc(mix_done, 1)

            def mixture_low(t):
                dve.wait_ge(mix_hi, t + 1)
                dve.tensor_tensor(tile(s_lo, t), tile(SG, t), tile(s_hi, t).bitcast(F32),
                                  ALU.subtract).then_inc(mix_lo, 1)

            tile_low(0, 0)
            for t in range(2):
                mixture_terms(t)
                if t == 0:
                    tile_low(1, 1)
                mixture_sum(t)
            finish1(GROUPS - 1)
            tile_low(2, 0)
            with dve.Fori(1, TILES // 2 - 1) as u:
                for b in range(2):
                    mixture_terms(u * 2 + b)
                    tile_low(u * 2 + (b + 1), (b + 1) % 2)
                    mixture_sum(u * 2 + b)
                    mixture_low(u * 2 + (b - 2))
            for t in (TILES - 2, TILES - 1):
                mixture_terms(t)
                if t == TILES - 2:
                    tile_low(TILES - 1, 1)
                mixture_sum(t)
                mixture_low(t - 2)
            mixture_low(TILES - 2)
            mixture_low(TILES - 1)

            def residual2(g):
                e = g + 2 * GROUPS
                dve.wait_ge(x_done, e)
                dve.wait_ge(nat_done, e + 1)
                dve.scalar_tensor_tensor(out=flat_y, in0=nat[:, :], scalar=0.0, in1=group(XA, g),
                                         op0=ALU.max, op1=ALU.add).then_inc(nat_read, 1)

            def h_low(g):
                dve.wait_ge(small_saved, g + (GROUPS + 1))
                dve.tensor_tensor(group(h_lo, g), turn[:, 0, :], group(h_hi, g).bitcast(F32),
                                  ALU.subtract).then_inc(h_lo_done, 1)

            def out2(g):
                dve.wait_ge(xT_done, g + GROUPS)
                dve.wait_ge(xn_kept, g + GROUPS)
                norm_out(g + 2 * GROUPS, in_xn)

            def layer2(g):
                first = isinstance(g, int)
                for c in range(CHUNKS):
                    low(c, (g - 4) * ROUND + (CUT2 + 2 * c))
                    if c == 1 and not first:
                        h_low(g - 5)
                    if c == 2:
                        residual2(g - 4)
                    if c == 3:
                        dve.wait_ge(nat_read, g + (2 * GROUPS - 3))
                        norm_stats(g + (2 * GROUPS - 4))
                    if c == 4:
                        norm_var(g + (2 * GROUPS - 4))
                    if c == 5:
                        out2(g - 4)

            layer2(4)
            with dve.Fori(5, GROUPS) as g:
                layer2(g)
            for t in range(2 * RING):
                low(t % RING, CUT3 + 2 * t)
                k = 4 + t // 4
                if t % 4 == 0:
                    h_low(k - 1)
                if t % 4 == 1:
                    residual2(k)
                    dve.wait_ge(nat_read, k + 2 * GROUPS + 1)
                    norm_stats(k + 2 * GROUPS)
                if t % 4 == 2:
                    norm_var(k + 2 * GROUPS)
                    out2(k)
            h_low(7)
            with dve.Fori(2, 4) as m:
                for c in range(CHUNKS):
                    low(c, m * ROUND + (CUT3 + 2 * c))

            def residual3(g):
                e = g + 3 * GROUPS
                dve.wait_ge(x_done, e)
                dve.wait_ge(nat_done, e + 1)
                dve.tensor_tensor(flat_y, nat[:, :], group(XA, g), ALU.add).then_inc(nat_read, 1)

            def stats3(g):
                dve.wait_ge(nat_read, g + (3 * GROUPS + 1))
                norm_stats(g + 3 * GROUPS)

            dve.wait_ge(xn_kept, 2 * GROUPS)

            def layer3(g, epilogues):
                for c in range(CHUNKS):
                    low(c, g * ROUND + (CUT3 + 2 * c))
                    if c >= 2 and (c - 2) // 3 < len(epilogues):
                        e = epilogues[(c - 2) // 3]
                        if c in (2, 5):
                            residual3(e)
                            stats3(e)
                        if c in (3, 6):
                            norm_var(e + 3 * GROUPS)
                        if c in (4, 7):
                            norm_out(e + 3 * GROUPS, in_place(e))

            with dve.Fori(4, GROUPS - 1) as g:
                layer3(g, [(g - 4) * 2, (g - 4) * 2 + 1])
            layer3(GROUPS - 1, [6])
            residual3(7)
            stats3(7)
            norm_var(7 + 3 * GROUPS)
            norm_out(7 + 3 * GROUPS, in_place(7))


_OUT = (GROUPS, GT, P, D)


def kernel(**inputs):
    import numpy as np
    import concourse.bacc as bacc
    from concourse.bass_utils import run_bass_kernel_spmd as run

    a = {k: np.asarray(v) for k, v in inputs.items()}
    adj = a["adj"]
    laid = {
        "x": a["x"].reshape(TILES, P, D).transpose(1, 0, 2).reshape(P, TILES * D),
        "adj_rows": adj.reshape(TILES, P, N),
        "adj_cols": adj.reshape(GROUPS, GN, TILES, P).transpose(0, 3, 2, 1).reshape(GROUPS, P, TILES * GN),
        "w_global": np.broadcast_to(a["L0_gnn_w_global"].reshape(1, 1), (P, 1)),
        "w_local": a["L0_gnn_w_local"].reshape(TILES, P).T,
        "w_agg": a["L0_gnn_W_agg"],
        "h_v": a["L1_gnn_H_v"],
        "w1": a["L2_gnn_W1"],
        "w2": a["L2_gnn_W2"].transpose(1, 0, 2).reshape(D, K * D),
        "b2": a["L2_gnn_b"],
        "w3t": a["L3_gnn_W"].T,
        "b3": a["L3_gnn_b"].reshape(1, D),
    }
    nc = bacc.Bacc("TRN2", target_bir_lowering=False, num_devices=1)
    arrays, args = {}, []
    for name, value in laid.items():
        value = np.ascontiguousarray(value)
        arrays[f"in_{name}"] = value
        args.append(nc.dram_tensor(f"in_{name}", value.shape, mybir.dt.from_np(value.dtype), kind="ExternalInput").ap())
    args.append(nc.dram_tensor("out", _OUT, F32, kind="ExternalOutput").ap())
    build(nc, *args)
    r = run(nc, [arrays], core_ids=[0])
    return r.results[0]["out"].reshape(N, D)
```

```python
from contextlib import ExitStack

import concourse.bass as bass
from concourse import mybir

F32 = mybir.dt.float32
F32R = mybir.dt.float32r
BF16 = mybir.dt.bfloat16
ALU = mybir.AluOpType
ACT = mybir.ActivationFunctionType

P = 128
N = 4096
D = 128
TILES = N // P
GT = 4
GN = GT * P
GROUPS = N // GN
SLOT = 2048
RING = 8
PN = 2 * P
CUT = SLOT // 2
ROUND = 2 * RING
CHUNKS = RING
K = 16
EPS = 1e-5
BIG = 2.0 ** 80


def build(nc, x, adj_rows, adj_cols, w_global, w_local, w_agg, h_v, w1, w2, b2, w3t, b3, out):
    with ExitStack() as ctx:
        def sb(name, shape, dt=F32):
            return ctx.enter_context(nc.sbuf_tensor(name, shape, dt))

        def sem(name):
            return ctx.enter_context(nc.semaphore(name))

        KB = 1024
        arena = nc.sbuf_usable_end // 32 * 32 - 176 * KB

        def at(name, at_kb, shape, dt=F32):
            return nc.alloc_sbuf_tensor_at(name, shape, dt, offset=arena + at_kb * KB)

        XA = at("XA", 0, [P, TILES * D])
        XB = at("XB", 16, [P, TILES * D])
        SG = at("SG", 32, [P, TILES * D])
        h_hi = at("h_hi", 16, [P, TILES * D], F32R)
        h_lo = at("h_lo", 32, [P, TILES * D], F32R)
        w_hi = at("w_hi", 16, [P, 2, CUT], F32R)
        w_lo = at("w_lo", 24, [P, 2, CUT], F32R)
        ring = at("ring", 48, [P, RING, SLOT])
        eT = at("eT", 112, [P, 2, TILES, PN])
        a_hi = at("a_hi", 112, [P, 4, CUT], F32R)
        a_lo = at("a_lo", 128, [P, 4, CUT], F32R)
        w2_hi = at("w2_hi", 112, [D, K * D], F32R)
        w2_lo = at("w2_lo", 120, [D, K * D], F32R)
        terms = at("terms", 128, [P, 2, K, D])
        s_hi = at("s_hi", 144, [P, TILES * D], F32R)
        s_lo = at("s_lo", 160, [P, TILES * D], F32R)

        first_odd = at("first_odd", 144, [P, N], BF16)[:, :]
        w2_sb = sb("w2_sb", [P, K * D])
        acc_sb = sb("acc_sb", [P, 5, GN])
        xT_sb = acc_sb[:, 3, :]
        ACC_PLACES = (4, 0, 1, 2)
        penalties = (w2_sb[:, :].bitcast(BF16), acc_sb[:, 0:4, :].rearrange("p a n -> p (a n)").bitcast(BF16))
        y = sb("y", [P, GT, D])
        xn = sb("xn", [P, GT, D])
        tT_hi = sb("tT_hi", [P, 2, P], F32R)
        tT_lo = sb("tT_lo", [P, 2, P], F32R)
        ident = sb("ident", [P, P])
        wagg_sb = sb("wagg_sb", [D, D])
        w3t_sb = sb("w3t_sb", [D, D])
        w1_sb = sb("w1_sb", [D, K])
        w1_hi = sb("w1_hi", [D, K], F32R)
        w1_lo = sb("w1_lo", [D, K], F32R)
        b2_sb = sb("b2_sb", [K, D])
        b3_sb = sb("b3_sb", [1, D])
        b3_hi = sb("b3_hi", [1, D], F32R)
        b3_lo = sb("b3_lo", [1, D], F32R)
        ones_row = sb("ones_row", [1, P], F32R)
        hv_sb = sb("hv_sb", [D, 1])
        hv_wide = sb("hv_wide", [D, P])
        gate = sb("gate", [P, TILES + 1])
        gate4 = sb("gate4", [P, GT])
        gate_x = sb("gate_x", [P, GT])
        stats = sb("stats", [P, GT, 6])
        mv = sb("mv", [P, GT, 2])
        var4 = sb("var4", [P, GT])
        rstd = sb("rstd", [P, GT])
        shift = sb("shift", [P, GT])
        minus_half = sb("minus_half", [P, GT])
        row_max = sb("row_max", [P, GT])
        neg_max = sb("neg_max", [P, GT])
        row_sum = sb("row_sum", [P, GT])
        has_edge = sb("has_edge", [P, GT])
        inv_sum = sb("inv_sum", [P, GT])
        node_all = sb("node_all", [P, TILES * K])
        node_cur = sb("node_cur", [P, 2, K])
        node4 = sb("node4", [P, GT * K])
        nodeT_sb = w2_sb[0:K, 0:GN]

        assert nc.sbuf_base <= arena

        acc = ctx.enter_context(nc.psum_tensor("acc", [P, 4, GN], F32))
        turn = ctx.enter_context(nc.psum_tensor("turn", [P, 2, GN], F32))
        nat = ctx.enter_context(nc.psum_tensor("nat", [P, GN], F32))
        xT = ctx.enter_context(nc.psum_tensor("xT", [P, GN], F32))
        nodeps = nat[:, 0:K]

        landed = [sem(f"landed{i}") for i in range(RING)]
        x_landed = [sem(f"x_landed{i}") for i in range(CHUNKS)]
        first_piece = sem("first_piece")
        small_landed = sem("small_landed")
        w2_landed = sem("w2_landed")
        stored = sem("stored")
        hi_done = sem("hi_done")
        lo_done = sem("lo_done")
        used = sem("used")
        x_hi_done = sem("x_hi_done")
        x_lo_done = sem("x_lo_done")
        bank0_done = sem("bank0_done")
        ident_zero = sem("ident_zero")
        consts = sem("consts")
        gate_exp = sem("gate_exp")
        gate_step = sem("gate_step")
        hv_ready = sem("hv_ready")
        w1_hi_done = sem("w1_hi_done")
        w1_cut = sem("w1_cut")
        ones_done = sem("ones_done")
        b3_hi_done = sem("b3_hi_done")
        b3_cut = sem("b3_cut")
        acc_saved = sem("acc_saved")
        nat_done = sem("nat_done")
        nat_read = sem("nat_read")
        gates_ready = sem("gates_ready")
        y_done = sem("y_done")
        stats_done = sem("stats_done")
        aggr_done = sem("aggr_done")
        var_done = sem("var_done")
        rstd_done = sem("rstd_done")
        shift_done = sem("shift_done")
        x_done = sem("x_done")
        xT_done = sem("xT_done")
        xT_saved = sem("xT_saved")
        xn_kept = sem("xn_kept")
        small_done = sem("small_done")
        small_saved = sem("small_saved")
        h_lo_done = sem("h_lo_done")
        pen_done = sem("pen_done")
        scaled = sem("scaled")
        max_done = sem("max_done")
        negmax_done = sem("negmax_done")
        exp_done = sem("exp_done")
        turned = sem("turned")
        evicted = sem("evicted")
        weighed = sem("weighed")
        waited = sem("waited")
        edge_done = sem("edge_done")
        recip_done = sem("recip_done")
        inv_done = sem("inv_done")
        w2_hi_done = sem("w2_hi_done")
        w2_cut = sem("w2_cut")
        p_xT = sem("p_xT")
        p_hi = sem("p_hi")
        p_lo = sem("p_lo")
        p_node = sem("p_node")
        p_node_saved = sem("p_node_saved")
        p_hw = sem("p_hw")
        p_even = sem("p_even")
        p_odd = sem("p_odd")
        mix_done = sem("mix_done")
        mix_hi = sem("mix_hi")
        mix_lo = sem("mix_lo")
        wide_hi = sem("wide_hi")
        wide_lo = sem("wide_lo")
        node4_done = sem("node4_done")
        nodeT_done = sem("nodeT_done")
        nodeT_saved = sem("nodeT_saved")

        LATE = 6
        CUT2 = GROUPS * ROUND
        CUT3 = CUT2 + 4 * ROUND
        USED2 = CUT2
        USED2B = USED2 + TILES
        USED3 = USED2B + 4 * ROUND

        def cols(buf, start, width):
            return buf[:, start:start + width] if isinstance(start, int) else buf[:, bass.ds(start, width)]

        def tile(buf, t):
            return cols(buf, t * D, D)

        def group(buf, g):
            return cols(buf, g * GN, GN)

        def bank_of(b):
            return acc[:, b, :] if isinstance(b, int) else acc[:, bass.ds(b, 1), :].rearrange("p o n -> p (o n)")

        def pair(r):
            return ring[:, 2 * r:2 * r + 2, :].rearrange("p a n -> p (a n)")

        block = ctx.enter_context(nc.Block())

        @block.sync
        def _(sp):
            def load(c, src, after=None, value=None):
                if after is not None:
                    sp.wait_ge(after, value)
                sp.dma_start(ring[:, c, :].rearrange("p (a n) -> p a n", a=src.shape[1]), src).then_inc(landed[c], 16)

            def columns(g, c):
                if isinstance(g, int):
                    return adj_cols[g:g + 1, :, c * SLOT:(c + 1) * SLOT].rearrange("o p n -> p o n")
                return adj_cols[bass.ds(g, 1), :, c * SLOT:(c + 1) * SLOT].rearrange("o p n -> p o n")

            def wide(t):
                part = slice(t * GN, (t + 1) * GN) if isinstance(t, int) else bass.ds(t * GN, GN)
                return adj_cols[0:4, :, part].rearrange("g p n -> p g n")

            def rows(t, half):
                return adj_rows[bass.ds(t, 1), :, half * SLOT:(half + 1) * SLOT].rearrange("o p n -> p o n")

            for c in range(CHUNKS):
                sp.dma_start(group(XA, c), group(x, c)).then_inc(x_landed[c], 16)
                if c == 0:
                    sp.dma_start(ring[:, 0, 0:CUT], adj_cols[0, :, 0:CUT]).then_inc(first_piece, 16)
                    sp.dma_start(ring[:, 0, CUT:SLOT], adj_cols[0, :, CUT:SLOT]).then_inc(landed[0], 16)
                else:
                    load(c, columns(0, c))
            for dst, src in ((wagg_sb[:, :], w_agg), (gate[:, 0:TILES], w_local), (gate[:, TILES:TILES + 1], w_global),
                             (hv_sb[:, :], h_v), (w1_sb[:, :], w1), (b2_sb[:, :], b2), (w3t_sb[:, :], w3t),
                             (b3_sb[:, :], b3)):
                sp.dma_start(dst, src).then_inc(small_landed, 16)
            with sp.Fori(1, GROUPS) as g:
                for c in range(CHUNKS):
                    load(c, columns(g, c), lo_done, g * ROUND + (2 * (c + 1) - ROUND))
            for c in range(CHUNKS):
                load(c, rows(c // 2, c % 2), lo_done, (GROUPS - 1) * ROUND + 2 * (c + 1))
            with sp.Fori(1, GROUPS) as g:
                for c in range(CHUNKS):
                    load(c, rows(g * GT + c // 2, c % 2), turned, (g - 1) * (GT * CHUNKS) + 4 * (c + 1))
            sp.wait_ge(max_done, TILES)
            sp.dma_start(w2_sb[:, :], w2).then_inc(w2_landed, 16)
            for c in range(CHUNKS):
                load(c, wide(c), turned, (GROUPS - 1) * (GT * CHUNKS) + 4 * (c + 1))
            with sp.Fori(1, 4) as m:
                for c in range(CHUNKS):
                    load(c, wide(m * CHUNKS + c), used, (m - 1) * RING + (USED2 + c + 1))
            for c in range(CHUNKS):
                load(c, columns(4, c), used, 3 * RING + (USED2 + c + 1))
            with sp.Fori(5, GROUPS) as g:
                for c in range(CHUNKS):
                    load(c, columns(g, c), lo_done, (g - 5) * ROUND + (CUT2 + 2 * (c + 1)))
            with sp.Fori(0, 4) as m:
                for c in range(CHUNKS):
                    load(c, wide(m * CHUNKS + c), lo_done, m * ROUND + (CUT3 - ROUND + 2 * (c + 1)))
            with sp.Fori(4, GROUPS) as g:
                for c in range(CHUNKS):
                    load(c, columns(g, c), lo_done, g * ROUND + (CUT3 - ROUND + 2 * (c + 1)))
            with sp.Fori(0, GROUPS) as g:
                sp.wait_ge(x_done, g + (3 * GROUPS + 1))
                sp.dma_start(out[bass.ds(g, 1), :, :, :].rearrange("o t p d -> p (o t) d"),
                             group(XA, g).rearrange("p (t d) -> p t d", d=D)).then_inc(stored, 16)
            sp.wait_ge(stored, 16 * GROUPS)

        @block.gpsimd
        def _(pool):
            pool.memset(ident[:, :], 0.0).then_inc(ident_zero, 1)
            pool.memset(minus_half[:, :], -0.5).then_inc(consts, 1)
            pool.wait_ge(ident_zero, 1)
            pool.affine_select(out=ident[:, :], in_=ident[:, :], compare_op=ALU.not_equal, fill=1.0, base=0,
                               pattern=[[-1, P]], channel_multiplier=1).then_inc(consts, 1)
            pool.wait_ge(consts, 2)
            with pool.Fori(0, 4 * GROUPS) as e:
                pool.wait_ge(var_done, e + 1)
                pool.tensor_tensor(rstd[:, :], var4[:, :], minus_half[:, :], ALU.pow).then_inc(rstd_done, 1)

        @block.scalar
        def _(act):
            def high(c, rounds, before, in_halves=False):
                for h in range(2):
                    if h == 0 and in_halves:
                        act.wait_ge(first_piece, 16)
                    else:
                        act.wait_ge(landed[c], rounds * 16)
                    if before is not None and not (isinstance(before, int) and before + h < 4):
                        act.wait_ge(used, before + (h - 3))
                    act.activation(a_hi[:, (2 * c + h) % 4, :], ring[:, c, h * CUT:(h + 1) * CUT],
                                   ACT.Copy).then_inc(hi_done, 1)

            def save_acc(complete, value, bank, k=0, turned_back=None):
                act.wait_ge(complete, value)
                if turned_back is not None:
                    act.wait_ge(nat_done, turned_back)
                act.activation(acc_sb[:, ACC_PLACES[k], :], bank, ACT.Copy).then_inc(acc_saved, 1)

            def norm_out(n, dst):
                act.wait_ge(shift_done, n + 1)
                for q in range(GT):
                    out_q = act.activation(dst(q), y[:, q, :], ACT.Identity, bias=shift[:, q:q + 1],
                                           scale=rstd[:, q:q + 1])
                out_q.then_inc(x_done, 1)

            def in_place(g):
                return lambda q: cols(XA, g * GN + q * D, D)

            def keep_xn(e, dst):
                act.wait_ge(x_done, e + 1)
                act.activation(dst, xn[:, :, :].rearrange("p t d -> p (t d)"), ACT.Copy).then_inc(xn_kept, 1)

            def save_xT(n, first=False):
                act.wait_ge(xT_done, n + 1)
                if not first:
                    act.wait_ge(small_done, n)
                act.activation(xT_sb, xT[:, :], ACT.Copy).then_inc(xT_saved, 1)

            def save_scores(g):
                act.wait_ge(small_done, g + 1)
                act.activation(group(SG, g), turn[:, 0, :], ACT.Copy, scale=1.0 / BIG).then_inc(small_saved, 1)

            def gated(g, first=False):
                if not first:
                    act.wait_ge(x_done, g)
                act.wait_ge(gates_ready, g + 1)
                act.wait_ge(nat_done, g + 1)
                for q in range(GT):
                    part = act.activation(y[:, q, :], nat[:, q * D:(q + 1) * D], ACT.Relu, scale=gate4[:, q:q + 1])
                part.then_inc(nat_read, 1)

            def norm0(g, first=False):
                if not first:
                    act.wait_ge(xT_done, g)
                    act.wait_ge(xn_kept, g)
                norm_out(g, lambda q: xn[:, q, :])

            for c in range(CHUNKS):
                act.wait_ge(x_landed[c], 16)
                act.activation(group(s_hi, c), group(XA, c), ACT.Copy).then_inc(x_hi_done, 1)
                high(c, 1, 2 * c, in_halves=c == 0)
            act.wait_ge(small_landed, 16 * 8)
            act.activation(gate[:, :], gate[:, :], ACT.Exp, scale=-1.0).then_inc(gate_exp, 1)
            act.activation(w1_hi[:, :], w1_sb[:, :], ACT.Copy).then_inc(w1_hi_done, 1)
            act.wait_ge(consts, 2)
            act.activation(ones_row[:, :], ident[0:1, :], ACT.Copy, scale=0.0, bias=1.0).then_inc(ones_done, 1)
            act.activation(b3_hi[:, :], b3_sb[:, :], ACT.Copy).then_inc(b3_hi_done, 1)

            def layer0(g, first=False, second=False):
                for c in range(CHUNKS):
                    high(c, g + 1, g * ROUND + 2 * c)
                    if c == 1 and not first:
                        save_xT(g - 2, first=second)
                    if c == 1:
                        save_acc(used, g * ROUND, bank_of(0 if first else (g - 1) % 4),
                                 turned_back=None if first else g - 1)
                    if c == 3:
                        gated(g - 1, first)
                    if c == 4 and not first:
                        save_scores(g - 2)
                    if c == 7:
                        norm0(g - 1, first)
                        keep_xn(g - 1, group(XB, g - 1))

            layer0(1, first=True)
            layer0(2, second=True)
            with act.Fori(3, GROUPS) as g:
                layer0(g)
            last = GROUPS - 1
            save_xT(last - 1)
            save_acc(used, GROUPS * ROUND, bank_of(last % 4), turned_back=last)
            save_scores(last - 1)
            gated(last)
            norm0(last)
            save_xT(last)
            save_scores(last)
            keep_xn(last, group(XB, last))

            def exponential(g, r, first=False):
                act.wait_ge(negmax_done, g * GT + (r + 1))
                if r == 0 and not first:
                    act.wait_ge(inv_done, g)
                act.activation(pair(r), pair(r), ACT.Exp, bias=neg_max[:, r:r + 1], scale=BIG,
                               accum_out=row_sum[:, r:r + 1]).then_inc(exp_done, 1)

            def evict(g, r):
                for c in range(CHUNKS):
                    act.wait_ge(turned, g * (GT * CHUNKS) + (r * CHUNKS + c + 1))
                    act.activation(eT[:, r // 2, 4 * c:4 * c + 4, (r % 2) * P:(r % 2 + 1) * P],
                                   turn[:, c % 2, :].rearrange("p (a n) -> p a n", a=4), ACT.Copy).then_inc(evicted, 1)

            def layer1(g, first=False, last=False, norm=True):
                for r in range(GT):
                    evict(g, r)
                    if r == 2 and norm:
                        norm_out(g + (GROUPS - 2), in_place(g - 2))
                    if r < GT - 1:
                        exponential(g, r + 1)
                    elif not last:
                        exponential(g + 1, 0)
                    if r == 1 and not first:
                        save_acc(weighed, g * 2, bank_of((g + 3) % 4), turned_back=g + (GROUPS - 1))

            exponential(0, 0, first=True)
            layer1(0, first=True, norm=False)
            layer1(1, norm=False)
            with act.Fori(2, GROUPS - 1) as g:
                layer1(g)
            layer1(GROUPS - 1, last=True)

            act.wait_ge(w2_landed, 16)
            act.wait_ge(weighed, 2 * GROUPS - 1)
            act.activation(w2_hi[:, :], w2_sb[:, :], ACT.Copy).then_inc(w2_hi_done, 1)

            def tile_high(t, b):
                act.wait_ge(p_xT, t + 1)
                if not (isinstance(t, int) and t < 2):
                    act.wait_ge(p_hw, t * 4 - 4)
                act.activation(tT_hi[:, b, :], xT[:, 0:P], ACT.Copy).then_inc(p_hi, 1)

            def mixture_high(t):
                act.wait_ge(mix_done, t + 1)
                act.activation(tile(s_hi, t), tile(SG, t), ACT.Copy).then_inc(mix_hi, 1)

            def wide_high(u, slot, t):
                act.wait_ge(landed[slot], u * 16 + (2 * GROUPS + 1) * 16)
                if isinstance(t, int) and t == 2:
                    act.wait_ge(nat_read, 2 * GROUPS)
                if not (isinstance(t, int) and t < 4):
                    act.wait_ge(used, t + (USED2 - 1))
                act.activation(w_hi[:, slot % 2, :], ring[:, slot, 0:CUT], ACT.Copy).then_inc(wide_hi, 1)

            def mixture_terms(t, b, between=None):
                act.wait_ge(p_node_saved, t + 1)
                if not (isinstance(t, int) and t < 2):
                    act.wait_ge(mix_done, t - 1)
                for c in (1, 3):
                    act.wait_ge(p_hw, t * 4 + (c + 1))
                    for k in range(4 * c, 4 * c + 4):
                        term = act.activation(terms[:, b, k, :], turn[:, 1, (k % 4) * D:(k % 4 + 1) * D], ACT.Copy,
                                              scale=node_cur[:, b, k:k + 1])
                    term.then_inc(p_odd, 1)
                    if c == 1 and between is not None:
                        between()

            def mixture(u, j):
                t = u * RING + j
                if not (isinstance(t, int) and t == TILES - 1):
                    tile_high(t + 1, (j + 1) % 2)
                mixture_high(t - 2)
                ahead = None
                if not (isinstance(t, int) and t < 3):
                    ahead = lambda: wide_high(u - (j == 0), (j - 1) % RING, t - 1)
                mixture_terms(t, j % 2, ahead)

            tile_high(0, 0)
            tile_high(1, 1)
            mixture_terms(0, 0)
            mixture_terms(1, 1)
            save_acc(weighed, 2 * GROUPS, acc[:, 3, :], turned_back=2 * GROUPS - 1)
            tile_high(2, 0)
            for j in range(2, RING):
                mixture(0, j)
            with act.Fori(1, TILES // RING - 1) as u:
                for j in range(RING):
                    mixture(u, j)

            def node_in(g, first=False):
                if not first:
                    act.wait_ge(nodeT_done, g)
                act.activation(node4[:, :], cols(node_all, g * (GT * K), GT * K), ACT.Copy).then_inc(node4_done, 1)

            def node_turned(g, first=False):
                act.wait_ge(nodeT_done, g + 1)
                if not first:
                    act.wait_ge(nat_done, g + 2 * GROUPS)
                act.activation(nodeT_sb[:, :], turn[0:K, 1, :], ACT.Copy).then_inc(nodeT_saved, 1)

            def h_high(g):
                act.wait_ge(small_done, g + (GROUPS + 1))
                act.activation(group(h_hi, g), turn[:, 0, :], ACT.Copy).then_inc(small_saved, 1)

            def layer2(g):
                first = isinstance(g, int)
                for c in range(CHUNKS):
                    high(c, g + 17, None if first and c < 2 else (g - 4) * ROUND + (USED2B + 2 * c))
                    if c == 0 and first:
                        save_acc(bank0_done, 1, acc[:, 0, :], turned_back=2 * GROUPS)
                    if c == 0 and not first:
                        save_xT(g - 5 + GROUPS)
                    if c == 5:
                        save_acc(used, (g - 4) * ROUND + USED2B, bank_of(g - 3 if first else (g - 3) % 4),
                                 turned_back=g - 3 + 2 * GROUPS)
                    if c == 2:
                        node_in(g - 3)
                    if c == 3 and not first:
                        h_high(g - 5)
                    if c == 5:
                        node_turned(g - 3)
                    if c == 7:
                        keep_xn(g - 4 + 2 * GROUPS, group(XA, g - 4))

            for j in range(RING):
                if j == RING - 1:
                    node_in(0, first=True)
                mixture(TILES // RING - 1, j)
            mixture_high(TILES - 2)
            wide_high(TILES // RING - 1, RING - 1, TILES - 1)
            mixture_high(TILES - 1)
            act.wait_ge(p_hw, 4 * TILES)
            node_turned(0, first=True)
            layer2(4)
            with act.Fori(5, GROUPS) as g:
                layer2(g)

            for k in range(1, 3):
                save_acc(used, USED2B + (k + 1) * ROUND, acc[:, k, :], k)
            for t in range(TILES):
                high(t % RING, 25 + t // RING, USED3 + 2 * t)
                if t == 0:
                    save_acc(used, USED3, acc[:, 3, :], 3)
                for k in range(3, GROUPS):
                    at = t - LATE * (k - 4)
                    if at == 2 and 4 <= k < GROUPS - 1:
                        node_in(k + 1)
                    if at == 5 and 4 <= k < GROUPS - 1:
                        node_turned(k + 1)
                    if at == 6 and k >= 4:
                        keep_xn(k + 2 * GROUPS, group(XA, k))
                    if at == 7:
                        save_xT(k + GROUPS)
                    if at == 10:
                        h_high(k)
            shifts = 2 * GROUPS - 2

            def layer3(g, first=False):
                e = (g - 4) * 2
                for c in range(CHUNKS):
                    high(c, g + 25, g * ROUND + (USED3 + 2 * c))
                    if c in (0, 3):
                        early = 1 if first and c == 0 else 0
                        save_acc(used, g * ROUND + USED3 - early, bank_of((e + c // 3) % 4), c // 3,
                                 turned_back=e + (3 * GROUPS - 1 + c // 3))
                    if c == 2 and not first:
                        norm_out(e + (shifts - 1), in_place(e - 1))
                    if c == 6:
                        norm_out(e + shifts, in_place(e))

            layer3(4, first=True)
            with act.Fori(5, GROUPS - 1) as g:
                layer3(g)
            for c in range(CHUNKS):
                high(c, GROUPS - 1 + 25, (GROUPS - 1) * ROUND + (USED3 + 2 * c))
                if c == 0:
                    save_acc(used, USED3 + 7 * ROUND, acc[:, 2, :], 2)
                if c == 2:
                    norm_out(5 + shifts, in_place(5))
                if c == 6:
                    norm_out(6 + shifts, in_place(6))
            save_acc(used, USED3 + 8 * ROUND, acc[:, 3, :], 3)

        @block.tensor
        def _(pe):
            pe.wait_ge(consts, 2)

            def three(dst, x_hi, x_lo, m_hi, m_lo, start, stop):
                pe.matmul(dst, x_hi, m_hi, start=start, stop=False)
                pe.matmul(dst, x_hi, m_lo, start=False, stop=False)
                return pe.matmul(dst, x_lo, m_hi, start=False, stop=stop)

            def group_chunk(cut, c, hi, lo, bank):
                for h in range(2):
                    pe.wait_ge(lo_done, cut + (h + 1))
                    b = (2 * c + h) % 4
                    for a in range(2):
                        t = 4 * c + 2 * h + a
                        mm = three(bank, tile(hi, t), tile(lo, t), a_hi[:, b, a * GN:(a + 1) * GN],
                                   a_lo[:, b, a * GN:(a + 1) * GN], t == 0, t == TILES - 1)
                    mm.then_inc(used, 1)

            def turn_back(e, k, weight=None, extra=False):
                pe.wait_ge(acc_saved, e + 1)
                if not (isinstance(e, int) and e == 0):
                    pe.wait_ge(nat_read, e)
                for q in range(GT):
                    if weight is None:
                        mm = pe.transpose(nat[:, q * D:(q + 1) * D], acc_sb[:, ACC_PLACES[k], q * P:(q + 1) * P], ident[:, :])
                        continue
                    mm = pe.matmul(nat[:, q * D:(q + 1) * D], acc_sb[:, ACC_PLACES[k], q * P:(q + 1) * P], weight[:, :],
                                   start=True, stop=not extra)
                    if extra:
                        mm = pe.matmul(nat[:, q * D:(q + 1) * D], nodeT_sb[:, q * P:(q + 1) * P], b2_sb[:, :],
                                       start=False, stop=True)
                mm.then_inc(nat_done, 1)

            def turn_x(e):
                pe.wait_ge(x_done, e + 1)
                for q in range(GT):
                    mm = pe.transpose(xT[:, q * P:(q + 1) * P], xn[:, q, :], ident[:, :])
                mm.then_inc(xT_done, 1)

            def scores(g, peeled=False):
                pe.wait_ge(xT_saved, g + 1)
                if not peeled:
                    pe.wait_ge(small_saved, g)
                pe.matmul(turn[:, 0, :], hv_wide[:, :], xT_sb, start=True, stop=True).then_inc(small_done, 1)

            for c in range(CHUNKS):
                pe.wait_ge(x_lo_done, c + 1)
                group_chunk(2 * c, c, s_hi, s_lo, acc[:, 0, :])
            pe.wait_ge(small_landed, 16 * 8)
            pe.wait_ge(hv_ready, 1)

            def layer0(g, four_ago=True, first=False):
                if four_ago:
                    pe.wait_ge(acc_saved, g - 3)
                for c in range(CHUNKS):
                    group_chunk(g * ROUND + 2 * c, c, s_hi, s_lo, bank_of(g % 4))
                    if c == 0:
                        turn_back(g - 1, 0, wagg_sb)
                    if c == 2 and not first:
                        scores(g - 2, peeled=isinstance(g, int) and g == 2)
                    if c == 7:
                        turn_x(g - 1)

            layer0(1, four_ago=False, first=True)
            layer0(2, four_ago=False)
            layer0(3, four_ago=False)
            with pe.Fori(4, GROUPS) as g:
                layer0(g)
            scores(GROUPS - 2)
            turn_back(GROUPS - 1, 0, wagg_sb)
            turn_x(GROUPS - 1)
            scores(GROUPS - 1)
            pe.wait_ge(small_saved, GROUPS)

            def turn_rows(g, r, c):
                if c == 0:
                    pe.wait_ge(exp_done, g * GT + (r + 1))
                if not (isinstance(g, int) and g == 0 and r == 0 and c < 2):
                    pe.wait_ge(evicted, g * (GT * CHUNKS) + (r * CHUNKS + c - 1))
                for a in range(4):
                    mm = pe.transpose(turn[:, c % 2, a * P:(a + 1) * P],
                                      pair(r)[:, (4 * c + a) * P:(4 * c + a + 1) * P], ident[:, :])
                mm.then_inc(turned, 1)

            def weigh(g, half, ts, bank):
                for t in ts:
                    if t == 0 and half == 0:
                        pe.wait_ge(acc_saved, g + (GROUPS - 3))
                    if t % 4 == 0:
                        pe.wait_ge(evicted, g * (GT * CHUNKS) + ((2 * half + 1) * CHUNKS + t // 4 + 1))
                    mm = pe.matmul(bank[:, half * PN:(half + 1) * PN], tile(XB, t), eT[:, half, t, :],
                                   start=(t == 0), stop=(t == TILES - 1))
                    if t == TILES - 1:
                        mm.then_inc(weighed, 1)

            def weigh_two(g, start, end):
                weigh(g - 1, 1, range(start, min(end, TILES)), bank_of((g + 3) % 4))
                weigh(g, 0, range(max(start, TILES) - TILES, end - TILES), bank_of(g % 4))

            def layer1(g, first=False, ends=(16, 32, 48, 64)):
                for r in range(GT):
                    start = 0 if r == 0 else ends[r - 1]
                    for c in range(CHUNKS):
                        turn_rows(g, r, c)
                        if not (first and r < 2):
                            at = min(start + c, ends[r])
                            weigh_two(g, at, min(at + 1, ends[r]) if c < CHUNKS - 1 else ends[r])
                    if r == 2 and not first:
                        turn_back(g + (GROUPS - 1), 0)

            pe.wait_ge(xn_kept, GROUPS)
            layer1(0, first=True)
            with pe.Fori(1, GROUPS - 1) as g:
                layer1(g)
            layer1(GROUPS - 1, ends=(20, 40, 60, 64))

            def turn_node(g):
                pe.wait_ge(node4_done, g + 1)
                if not (isinstance(g, int) and g == 0):
                    pe.wait_ge(nodeT_saved, g)
                for q in range(GT):
                    mm = pe.transpose(turn[0:K, 1, q * P:(q + 1) * P], node4[:, q * K:(q + 1) * K], ident[:, :])
                mm.then_inc(nodeT_done, 1)

            def turn_tile(t):
                if t >= TILES - GT:
                    pe.wait_ge(x_done, 2 * GROUPS)
                elif t == 0:
                    pe.wait_ge(x_done, 2 * GROUPS - 2)
                elif t == TILES - 2 * GT:
                    pe.wait_ge(x_done, 2 * GROUPS - 1)
                if t >= 1:
                    pe.wait_ge(p_lo, t)
                pe.transpose(xT[:, 0:P], tile(XA, t), ident[:, :]).then_inc(p_xT, 1)

            def node(t):
                pe.wait_ge(p_lo, t + 1)
                if t >= 1:
                    pe.wait_ge(p_node_saved, t)
                if t == 0:
                    pe.wait_ge(nat_read, 2 * GROUPS - 1)
                if t == 2:
                    pe.wait_ge(nat_read, 2 * GROUPS)
                three(nodeps, tT_hi[:, t % 2, :], tT_lo[:, t % 2, :], w1_hi[:, :], w1_lo[:, :], True, True).then_inc(p_node, 1)

            def bases(t, c):
                n = 4 * t + c
                if n >= 2:
                    pe.wait_ge((p_even, p_odd)[c % 2], n // 2)
                part = slice(c * GN, (c + 1) * GN)
                three(turn[:, c % 2, :], tT_hi[:, t % 2, :], tT_lo[:, t % 2, :], w2_hi[:, part], w2_lo[:, part],
                      True, True).then_inc(p_hw, 1)

            def last_pair(start, end):
                weigh(GROUPS - 1, 1, range(start, end), acc[:, 3, :])

            turn_tile(0)
            last_pair(0, 10)
            pe.wait_ge(w1_cut, 1)
            pe.wait_ge(w2_cut, 1)
            turn_tile(1)
            done = 10
            for t in range(2):
                node(t)
                for c in range(4):
                    last_pair(done, done + 2)
                    done += 2
                    bases(t, c)
            last_pair(done, TILES)
            pe.wait_ge(p_node_saved, 2)
            turn_tile(2)
            turn_back(2 * GROUPS - 1, 0)
            for t in range(TILES):
                if t == TILES - 1:
                    pe.wait_ge(p_odd, 2 * TILES)
                    turn_node(0)
                if t + 3 < TILES:
                    turn_tile(t + 3)
                pe.wait_ge(landed[t % RING], 16 * (2 * GROUPS + t // RING + 1))
                pe.wait_ge(mix_done, t + 1)
                for i, k in enumerate((2, 3, 0, 1)):
                    if t < 2 or k >= 2:
                        mm = pe.matmul(acc[:, k, :], tile(SG, t), ring[:, t % RING, k * GN:(k + 1) * GN],
                                       start=(t == 0), stop=(t == TILES - 1))
                    else:
                        if k == 0:
                            pe.wait_ge(wide_lo, t - 1)
                            pe.wait_ge(mix_lo, t + 1)
                        part = slice(k * GN, (k + 1) * GN)
                        mm = three(acc[:, k, :], tile(s_hi, t), tile(s_lo, t), w_hi[:, t % 2, part],
                                   w_lo[:, t % 2, part], False, t == TILES - 1)
                    if k == 0 and t == TILES - 1:
                        mm.then_inc(bank0_done, 1)
                    if k == 1:
                        mm.then_inc(used, 1)
                    if t + 2 < TILES:
                        if i == 0:
                            node(t + 2)
                        bases(t + 2, i)

            def project(g, first=False):
                pe.wait_ge(xT_saved, g + (GROUPS + 1))
                pe.wait_ge(small_saved, g + GROUPS)
                if not first:
                    pe.wait_ge(h_lo_done, g)
                for i, part in enumerate((b3_hi, b3_lo)):
                    pe.matmul(turn[:, 0, :].rearrange("p (q d) -> p q d", d=D), ones_row[:, :],
                              part[:, :].rearrange("o (q d) -> o q d", q=1).to_broadcast([1, GT, D]),
                              start=i == 0, stop=False)
                for q in range(GT):
                    mm = pe.matmul(turn[:, 0, q * D:(q + 1) * D], xT_sb[:, q * P:(q + 1) * P], w3t_sb[:, :],
                                   start=False, stop=q == GT - 1)
                mm.then_inc(small_done, 1)

            pe.wait_ge(ones_done, 1)
            pe.wait_ge(b3_cut, 1)

            def layer2(g, first=False, second=False):
                for c in range(CHUNKS):
                    if c == 0:
                        pe.wait_ge(acc_saved, g + (2 * GROUPS - 3))
                    group_chunk((g - 4) * ROUND + (CUT2 + 2 * c), c, s_hi, s_lo, bank_of(g - 4))
                    if c == 0:
                        pe.wait_ge(nodeT_saved, g - 3)
                        turn_back(g + (2 * GROUPS - 4), 0, ident, extra=True)
                    if c == 1 and not first:
                        project(g - 5, first=second)
                    if c == 3:
                        turn_node(g - 3)
                    if c == 6:
                        turn_x(g + (2 * GROUPS - 4))

            layer2(4, first=True)
            layer2(5, second=True)
            with pe.Fori(6, GROUPS) as g:
                layer2(g)

            for t in range(TILES):
                if t % 4 == 0:
                    pe.wait_ge(h_lo_done, t // GT + 1)
                for h in range(2):
                    if t == 0:
                        pe.wait_ge(acc_saved, 3 * GROUPS - 1 + h)
                    pe.wait_ge(lo_done, CUT3 + 2 * t + h + 1)
                    for a, (still, moving) in enumerate(((h_hi, a_hi), (h_hi, a_lo), (h_lo, a_hi))):
                        for b in range(2):
                            mm = pe.matmul(acc[:, 2 * h + b, :], tile(still, t),
                                           moving[:, (2 * t + h) % 4, b * GN:(b + 1) * GN],
                                           start=(t == 0 and a == 0), stop=(t == TILES - 1 and a == 2))
                    mm.then_inc(used, 1)
                for k in range(3, GROUPS):
                    at = t - LATE * (k - 4)
                    if at == 0 and k >= 4:
                        pe.wait_ge(nodeT_saved, k + 1)
                        turn_back(k + 2 * GROUPS, k - 4, ident, extra=True)
                    if at == 3 and 4 <= k < GROUPS - 1:
                        turn_node(k + 1)
                    if at == 5 and k >= 4:
                        turn_x(k + 2 * GROUPS)
                    if at == 8:
                        project(k)
            with pe.Fori(4, GROUPS - 1) as g:
                for c in range(CHUNKS):
                    if c == 0:
                        pe.wait_ge(acc_saved, g - 4 + (3 * GROUPS + 1))
                    group_chunk(g * ROUND + (CUT3 + 2 * c), c, h_hi, h_lo, bank_of(g - 4))
                    if c in (0, 4):
                        turn_back((g - 4) * 2 + (3 * GROUPS + c // 4), c // 4)
            for c in range(CHUNKS):
                if c == 0:
                    pe.wait_ge(acc_saved, 3 * GROUPS + 4)
                group_chunk((GROUPS - 1) * ROUND + (CUT3 + 2 * c), c, h_hi, h_lo, acc[:, 3, :])
                if c == 0:
                    turn_back(3 * GROUPS + 6, 2)
            turn_back(3 * GROUPS + 7, 3)

        @block.vector
        def _(dve):
            flat_y = y[:, :, :].rearrange("p t d -> p (t d)")

            def low(c, cut):
                for h in range(2):
                    b = (2 * c + h) % 4
                    dve.wait_ge(hi_done, cut + (h + 1))
                    dve.tensor_tensor(a_lo[:, b, :], ring[:, c, h * CUT:(h + 1) * CUT], a_hi[:, b, :].bitcast(F32),
                                      ALU.subtract).then_inc(lo_done, 1)

            def norm_stats(e):
                for q in range(GT):
                    bn = dve.bn_stats(stats[:, q, :], y[:, q, :])
                bn.then_inc(stats_done, 1)

            def norm_var(e):
                dve.wait_ge(stats_done, e + 1)
                dve.sem_inc(waited, 1)
                for q in range(GT):
                    bn = dve.bn_aggr(mv[:, q, :], stats[:, q, :])
                bn.then_inc(aggr_done, 1)
                dve.wait_ge(aggr_done, e + 1)
                dve.tensor_scalar(var4[:, :], mv[:, :, 1], EPS, None, ALU.add).then_inc(var_done, 1)

            def norm_shift(e):
                dve.wait_ge(rstd_done, e + 1)
                dve.scalar_tensor_tensor(out=shift[:, :], in0=mv[:, :, 0], scalar=-1.0, in1=rstd[:, :],
                                         op0=ALU.mult, op1=ALU.mult).then_inc(shift_done, 1)

            def norm_out(e, dst):
                dve.wait_ge(rstd_done, e + 1)
                for q in range(GT):
                    ts = dve.tensor_scalar(dst(q), y[:, q, :], mv[:, q, 0:1], rstd[:, q:q + 1],
                                           ALU.subtract, ALU.mult)
                ts.then_inc(x_done, 1)

            def in_xn(q):
                return xn[:, q, :]

            def in_place(g):
                return lambda q: cols(XA, g * GN + q * D, D)

            for c in range(CHUNKS):
                dve.wait_ge(x_hi_done, c + 1)
                dve.tensor_tensor(group(s_lo, c), group(XA, c), group(s_hi, c).bitcast(F32),
                                  ALU.subtract).then_inc(x_lo_done, 1)
                low(c, 2 * c)
            dve.wait_ge(small_landed, 16 * 8)
            dve.tensor_copy(hv_wide[:, :], hv_sb[:, 0:1].to_broadcast([D, P])).then_inc(hv_ready, 1)
            dve.wait_ge(w1_hi_done, 1)
            dve.tensor_tensor(w1_lo[:, :], w1_sb[:, :], w1_hi[:, :].bitcast(F32), ALU.subtract).then_inc(w1_cut, 1)
            dve.wait_ge(b3_hi_done, 1)
            dve.tensor_tensor(b3_lo[:, :], b3_sb[:, :], b3_hi[:, :].bitcast(F32), ALU.subtract).then_inc(b3_cut, 1)
            dve.wait_ge(gate_exp, 1)
            dve.tensor_scalar(gate[:, :], gate[:, :], 1.0, None, ALU.add).then_inc(gate_step, 1)
            dve.wait_ge(gate_step, 1)
            dve.reciprocal(gate[:, :], gate[:, :]).then_inc(gate_step, 1)
            dve.wait_ge(gate_step, 2)
            dve.tensor_scalar(gate[:, 0:TILES], gate[:, 0:TILES], gate[:, TILES:TILES + 1], None,
                              ALU.mult).then_inc(gate_step, 1)
            dve.wait_ge(gate_step, 3)

            def gates0(g):
                dve.tensor_scalar(gate_x[:, :], cols(gate, g * GT, GT), -1.0, 2.0, ALU.mult, ALU.add)
                dve.tensor_scalar(gate4[:, :], cols(gate, g * GT, GT), 1.0, None, ALU.mult).then_inc(gates_ready, 1)

            def residual0(g):
                dve.wait_ge(gates_ready, g + 1)
                dve.wait_ge(nat_read, g + 1)
                for q in range(GT):
                    st = dve.scalar_tensor_tensor(out=y[:, q, :], in0=cols(XA, g * GN + q * D, D),
                                                  scalar=gate_x[:, q:q + 1], in1=y[:, q, :],
                                                  op0=ALU.mult, op1=ALU.add)
                st.then_inc(y_done, 1)
                dve.wait_ge(y_done, g + 1)
                norm_stats(g)

            def layer0(g):
                first = isinstance(g, int)
                for c in range(CHUNKS):
                    low(c, g * ROUND + 2 * c)
                    if c == 1:
                        if not first:
                            dve.wait_ge(y_done, g - 1)
                        gates0(g - 1)
                    if c == 4:
                        residual0(g - 1)
                    if c == 5:
                        norm_var(g - 1)
                    if c == 6:
                        norm_shift(g - 1)

            layer0(1)
            with dve.Fori(2, GROUPS) as g:
                layer0(g)

            def mask(g, r, place=None):
                n = g * GT + r
                for half in range(2):
                    dve.wait_ge(landed[2 * r + half], (g + GROUPS + 1) * 16)
                if not (isinstance(g, int) and n < 2):
                    dve.wait_ge(max_done, n - 1)
                place = penalties[r % 2] if place is None else place
                dve.tensor_scalar(place, pair(r), 0.0, -1.0, ALU.is_equal, ALU.mult).then_inc(pen_done, 1)

            def times_scores(r, start, end):
                part = slice(start * GN, end * GN)
                return dve.tensor_tensor(pair(r)[:, part], pair(r)[:, part], SG[:, part], ALU.mult)

            def row_maxima(g, r, place=None):
                n = g * GT + r
                place = penalties[r % 2] if place is None else place
                dve.wait_ge(pen_done, n + 1)
                dve.wait_ge(scaled, n + 1)
                dve.sem_inc(waited, 1)
                dve.tensor_tensor_reduce(pair(r), pair(r), place, 1.0, -3.0e38, ALU.add, ALU.max,
                                         row_max[:, r:r + 1]).then_inc(max_done, 1)

            def negated(g, r):
                n = g * GT + r
                dve.wait_ge(max_done, n + 1)
                if not (isinstance(g, int) and g == 0):
                    dve.wait_ge(exp_done, n - (GT - 1))
                dve.tensor_scalar(neg_max[:, r:r + 1], row_max[:, r:r + 1], -BIG, None,
                                  ALU.mult).then_inc(negmax_done, 1)

            def logits(g, r, between=None):
                mask(g, r)
                if r > 0:
                    negated(g, r - 1)
                else:
                    negated(g - 1, GT - 1)
                    edges(g - 1)
                times_scores(r, 0, GROUPS).then_inc(scaled, 1)
                if between is not None:
                    between()
                row_maxima(g, r)

            def edges(g):
                if not (isinstance(g, int) and g == 0):
                    dve.wait_ge(inv_done, g)
                dve.tensor_scalar(has_edge[:, :], row_max[:, :], -0.5, None, ALU.is_gt).then_inc(edge_done, 1)

            def inverse(g):
                dve.wait_ge(exp_done, g * GT + GT)
                dve.wait_ge(edge_done, g + 1)
                dve.reciprocal(inv_sum[:, :], row_sum[:, :]).then_inc(recip_done, 1)
                dve.wait_ge(recip_done, g + 1)
                dve.tensor_tensor(inv_sum[:, :], inv_sum[:, :], has_edge[:, :], ALU.mult).then_inc(inv_done, 1)

            def residual1(g):
                e = g + GROUPS
                dve.wait_ge(x_done, e)
                dve.wait_ge(nat_done, e + 1)
                for q in range(GT):
                    st = dve.scalar_tensor_tensor(out=y[:, q, :], in0=nat[:, q * D:(q + 1) * D],
                                                  scalar=inv_sum[:, q:q + 1], in1=cols(XB, g * GN + q * D, D),
                                                  op0=ALU.mult, op1=ALU.add)
                st.then_inc(nat_read, 1)

            def stats1(g):
                dve.wait_ge(nat_read, g + (GROUPS + 1))
                norm_stats(g + GROUPS)

            def finish1(g):
                residual1(g)
                stats1(g)
                norm_var(g + GROUPS)
                norm_out(g + GROUPS, in_place(g))

            dve.wait_ge(y_done, GROUPS - 1)
            gates0(GROUPS - 1)
            mask(0, 0)
            dve.wait_ge(small_saved, 4)
            dve.wait_ge(pen_done, 1)
            times_scores(0, 0, 3)
            residual0(GROUPS - 1)
            norm_var(GROUPS - 1)
            times_scores(0, 3, 5)
            norm_shift(GROUPS - 1)
            dve.wait_ge(small_saved, GROUPS - 1)
            times_scores(0, 5, GROUPS - 1)
            mask(0, 1, first_odd)
            dve.wait_ge(small_saved, GROUPS)
            times_scores(0, GROUPS - 1, GROUPS).then_inc(scaled, 1)
            row_maxima(0, 0)
            negated(0, 0)
            times_scores(1, 0, GROUPS).then_inc(scaled, 1)
            row_maxima(0, 1, first_odd)
            for r in range(2, GT):
                logits(0, r)
            logits(1, 0, lambda: inverse(0))
            for r in range(1, GT):
                logits(1, r)
            dve.wait_ge(xn_kept, GROUPS)
            with dve.Fori(2, GROUPS) as g:
                def residual_and_inverse():
                    residual1(g - 2)
                    dve.wait_ge(nat_read, g + (GROUPS - 1))
                    inverse(g - 1)

                logits(g, 0, residual_and_inverse)
                logits(g, 1, lambda: stats1(g - 2))
                logits(g, 2, lambda: norm_var(g + (GROUPS - 2)))
                logits(g, 3, lambda: norm_shift(g + (GROUPS - 2)))
            negated(GROUPS - 1, GT - 1)
            edges(GROUPS - 1)
            finish1(GROUPS - 2)
            inverse(GROUPS - 1)

            dve.wait_ge(w2_hi_done, 1)
            dve.tensor_tensor(w2_lo[:, :], w2_sb[:, :], w2_hi[:, :].bitcast(F32), ALU.subtract).then_inc(w2_cut, 1)

            def tile_low(t, b):
                dve.wait_ge(p_hi, t + 1)
                dve.tensor_tensor(tT_lo[:, b, :], xT[:, 0:P], tT_hi[:, b, :].bitcast(F32),
                                  ALU.subtract).then_inc(p_lo, 1)

            def mixture_terms(t, b):
                first = isinstance(t, int) and t == 0
                dve.wait_ge(p_node, t + 1)
                dve.tensor_copy(node_cur[:, b, :], nodeps)
                dve.tensor_copy(cols(node_all, t * K, K), nodeps).then_inc(p_node_saved, 1)
                dve.wait_ge(p_node_saved, t + 1)
                for c in (0, 2):
                    dve.wait_ge(p_hw, t * 4 + (c + 1))
                    dve.tensor_tensor(terms[:, b, 4 * c:4 * c + 4, :],
                                      turn[:, c % 2, :].rearrange("p (k f) -> p k f", k=4),
                                      node_cur[:, b, 4 * c:4 * c + 4].rearrange("p (k o) -> p k o", o=1).to_broadcast([P, 4, D]),
                                      ALU.mult).then_inc(p_even, 1)
                    if c == 0 and not first:
                        mixture_sum(t - 1, (b + 1) % 2)

            def mixture_sum(t, b):
                dve.wait_ge(p_even, t * 2 + 2)
                dve.wait_ge(p_odd, t * 2 + 2)
                dve.tensor_reduce(tile(SG, t), terms[:, b, :, :].rearrange("p k f -> p f k"),
                                  mybir.AxisListType.X, ALU.add).then_inc(mix_done, 1)

            def mixture_low(t):
                dve.wait_ge(mix_hi, t + 1)
                dve.tensor_tensor(tile(s_lo, t), tile(SG, t), tile(s_hi, t).bitcast(F32),
                                  ALU.subtract).then_inc(mix_lo, 1)

            tile_low(0, 0)
            tile_low(1, 1)
            mixture_terms(0, 0)
            mixture_terms(1, 1)
            tile_low(2, 0)
            finish1(GROUPS - 1)

            def wide_low(t, slot):
                dve.wait_ge(wide_hi, t - 1)
                dve.tensor_tensor(w_lo[:, slot % 2, :], ring[:, slot, 0:CUT], w_hi[:, slot % 2, :].bitcast(F32),
                                  ALU.subtract).then_inc(wide_lo, 1)

            def mixture(u, j):
                t = u * RING + j
                if not (isinstance(t, int) and t < 4):
                    wide_low(t - 2, (j - 2) % RING)
                if not (isinstance(t, int) and t == TILES - 1):
                    tile_low(t + 1, (j + 1) % 2)
                mixture_low(t - 2)
                mixture_terms(t, j % 2)

            for j in range(2, RING):
                mixture(0, j)
            with dve.Fori(1, TILES // RING - 1) as u:
                for j in range(RING):
                    mixture(u, j)
            for j in range(RING):
                mixture(TILES // RING - 1, j)
            wide_low(TILES - 2, RING - 2)
            mixture_low(TILES - 2)
            mixture_sum(TILES - 1, 1)
            wide_low(TILES - 1, RING - 1)
            mixture_low(TILES - 1)

            def residual2(g):
                e = g + 2 * GROUPS
                dve.wait_ge(x_done, e)
                dve.wait_ge(nat_done, e + 1)
                dve.scalar_tensor_tensor(out=flat_y, in0=nat[:, :], scalar=0.0, in1=group(XA, g),
                                         op0=ALU.max, op1=ALU.add).then_inc(nat_read, 1)

            def h_low(g):
                dve.wait_ge(small_saved, g + (GROUPS + 1))
                dve.tensor_tensor(group(h_lo, g), turn[:, 0, :], group(h_hi, g).bitcast(F32),
                                  ALU.subtract).then_inc(h_lo_done, 1)

            def out2(g):
                dve.wait_ge(xT_done, g + GROUPS)
                dve.wait_ge(xn_kept, g + GROUPS)
                norm_out(g + 2 * GROUPS, in_xn)

            def layer2(g):
                first = isinstance(g, int)
                for c in range(CHUNKS):
                    low(c, (g - 4) * ROUND + (CUT2 + 2 * c))
                    if c == 3:
                        residual2(g - 4)
                    if c == 4:
                        dve.wait_ge(nat_read, g + (2 * GROUPS - 3))
                        norm_stats(g + (2 * GROUPS - 4))
                        if not first:
                            h_low(g - 5)
                    if c == 5:
                        norm_var(g + (2 * GROUPS - 4))
                    if c == 6:
                        out2(g - 4)

            dve.wait_ge(mix_done, TILES)
            layer2(4)
            with dve.Fori(5, GROUPS) as g:
                layer2(g)
            for t in range(TILES):
                low(t % RING, CUT3 + 2 * t)
                for k in range(3, GROUPS):
                    at = t - LATE * (k - 4)
                    e = k + 2 * GROUPS
                    if at == 3 and k >= 4:
                        residual2(k)
                        dve.wait_ge(nat_read, e + 1)
                        norm_stats(e)
                    if at == 4 and k >= 4:
                        norm_var(e)
                    if at == 5 and k >= 4:
                        out2(k)
                    if at == 10:
                        h_low(k)

            def residual3(g):
                e = g + 3 * GROUPS
                dve.wait_ge(x_done, e)
                dve.wait_ge(nat_done, e + 1)
                dve.tensor_tensor(flat_y, nat[:, :], group(XA, g), ALU.add).then_inc(nat_read, 1)

            def stats3(g):
                dve.wait_ge(nat_read, g + (3 * GROUPS + 1))
                norm_stats(g + 3 * GROUPS)

            dve.wait_ge(xn_kept, 2 * GROUPS)

            def layer3(g, earlier, e, f):
                for c in range(CHUNKS):
                    low(c, g * ROUND + (CUT3 + 2 * c))
                    if c == 0 and earlier is not None:
                        norm_var(earlier + 3 * GROUPS)
                    if c == 1 and earlier is not None:
                        norm_shift(earlier + 3 * GROUPS)
                    if c == 2:
                        residual3(e)
                    if c == 3:
                        stats3(e)
                    if c == 4:
                        norm_var(e + 3 * GROUPS)
                    if c == 5:
                        norm_shift(e + 3 * GROUPS)
                    if c == 6 and f is not None:
                        residual3(f)
                    if c == 7 and f is not None:
                        stats3(f)

            layer3(4, None, 0, 1)
            with dve.Fori(5, GROUPS - 1) as g:
                layer3(g, (g - 5) * 2 + 1, (g - 4) * 2, (g - 4) * 2 + 1)
            layer3(GROUPS - 1, 5, 6, None)
            residual3(7)
            stats3(7)
            norm_var(7 + 3 * GROUPS)
            norm_out(7 + 3 * GROUPS, in_place(7))


_OUT = (GROUPS, GT, P, D)


def kernel(**inputs):
    import numpy as np
    import concourse.bacc as bacc
    from concourse.bass_utils import run_bass_kernel_spmd as run

    a = {k: np.asarray(v) for k, v in inputs.items()}
    adj = a["adj"]
    laid = {
        "x": a["x"].reshape(TILES, P, D).transpose(1, 0, 2).reshape(P, TILES * D),
        "adj_rows": adj.reshape(TILES, P, N),
        "adj_cols": adj.reshape(GROUPS, GN, TILES, P).transpose(0, 3, 2, 1).reshape(GROUPS, P, TILES * GN),
        "w_global": np.broadcast_to(a["L0_gnn_w_global"].reshape(1, 1), (P, 1)),
        "w_local": a["L0_gnn_w_local"].reshape(TILES, P).T,
        "w_agg": a["L0_gnn_W_agg"],
        "h_v": a["L1_gnn_H_v"],
        "w1": a["L2_gnn_W1"],
        "w2": a["L2_gnn_W2"].transpose(1, 0, 2).reshape(D, K * D),
        "b2": a["L2_gnn_b"],
        "w3t": a["L3_gnn_W"].T,
        "b3": a["L3_gnn_b"].reshape(1, D),
    }
    nc = bacc.Bacc("TRN2", target_bir_lowering=False, num_devices=1)
    arrays, args = {}, []
    for name, value in laid.items():
        value = np.ascontiguousarray(value)
        arrays[f"in_{name}"] = value
        args.append(nc.dram_tensor(f"in_{name}", value.shape, mybir.dt.from_np(value.dtype), kind="ExternalInput").ap())
    args.append(nc.dram_tensor("out", _OUT, F32, kind="ExternalOutput").ap())
    build(nc, *args)
    r = run(nc, [arrays], core_ids=[0])
    return r.results[0]["out"].reshape(N, D)
```
